# Optimizing a Trainium2 kernel written in Bass

```python
import numpy as np
import jax
import jax.numpy as jnp

def _softmax(x, axis=-1):
    return jax.nn.softmax(x, axis=axis)

def _gelu(x):
    return jax.nn.gelu(x, approximate=True)

def _silu(x):
    return jax.nn.silu(x)

def _sigmoid(x):
    return jax.nn.sigmoid(x)

def _layernorm(x, axis=-1, eps=1e-05):
    m = jnp.mean(x, axis=axis, keepdims=True)
    v = jnp.var(x, axis=axis, keepdims=True)
    return (x - m) / jnp.sqrt(v + eps)

def _scatter_add(tgt, idx, src, axis=0):
    return tgt.at[idx].add(src)

def _segment_sum(src, seg, n):
    return jax.ops.segment_sum(src, seg, n)
kernel_name = 'mk_macaron_d1_jaxref_r4_376ae8'

def setup_inputs(seed: int=0):
    np.random.seed(seed)
    _w = jnp.asarray

    def _L0_attn_setup():
        import jax, jax.numpy as jnp
        import numpy as np
        EPS = 1e-06

        def _rms(x):
            return x * jax.lax.rsqrt(jnp.mean(x * x, axis=-1, keepdims=True) + EPS)
        key = jax.random.key(seed)
        ks = jax.random.split(key, 10)
        B, S, D, MULT = (4, 1024, 256, 4)
        H = MULT * D

        def w(k, shape, s=0.02):
            return jax.random.normal(k, shape, jnp.float32) * s
        return {'x': jax.random.normal(ks[0], (B, S, D), jnp.float32), 'Wk': w(ks[1], (D, D)), 'Wv': w(ks[2], (D, D)), 'Wr': w(ks[3], (D, D)), 'Wo': w(ks[4], (D, D)), 'time_decay': jax.random.normal(ks[5], (D,), jnp.float32) * 0.01 - 5.0, 'time_first': jax.random.normal(ks[6], (D,), jnp.float32) * 0.01, 'mixer_scale': jnp.ones((D,), jnp.float32), 'Wfc': w(ks[7], (H, D)), 'Wmlp': w(ks[8], (D, H)), 'mlp_scale': jnp.ones((D,), jnp.float32)}
    _L0_attn_in = _L0_attn_setup()

    def _L0_ffn_setup():
        import jax, jax.numpy as jnp
        import numpy as np
        import math
        DIM = 256
        NUM_HEADS = 16
        SHARED_HEADS = 1
        ROUTED_HEADS = 3
        HEAD_DIM = DIM // NUM_HEADS
        B, N = (2, 512)
        key = jax.random.key(seed)
        ks = jax.random.split(key, 16)
        s = 1.0 / math.sqrt(DIM)
        inp = {'x': jax.random.normal(ks[0], (B, N, DIM), dtype=jnp.float32), 'Wq': jax.random.uniform(ks[1], (DIM, DIM), minval=-s, maxval=s), 'bq': jax.random.uniform(ks[2], (DIM,), minval=-s, maxval=s), 'Wk': jax.random.uniform(ks[3], (DIM, DIM), minval=-s, maxval=s), 'bk': jax.random.uniform(ks[4], (DIM,), minval=-s, maxval=s), 'Wv': jax.random.uniform(ks[5], (DIM, DIM), minval=-s, maxval=s), 'bv': jax.random.uniform(ks[6], (DIM,), minval=-s, maxval=s), 'Wp': jax.random.uniform(ks[7], (DIM, DIM), minval=-s, maxval=s), 'bp': jax.random.uniform(ks[8], (DIM,), minval=-s, maxval=s), 'Wr': jax.random.uniform(ks[9], (NUM_HEADS - SHARED_HEADS, DIM), minval=-s, maxval=s), 'br': jax.random.uniform(ks[10], (NUM_HEADS - SHARED_HEADS,), minval=-s, maxval=s), 'Ws': jax.random.uniform(ks[11], (2, DIM), minval=-s, maxval=s), 'bs': jax.random.uniform(ks[12], (2,), minval=-s, maxval=s), 'temperature': jnp.full((NUM_HEADS, 1, 1), float(np.log(np.expm1(1.0 / 0.24))), dtype=jnp.float32), 'query_embedding': 0.02 * jax.random.normal(ks[13], (NUM_HEADS, 1, HEAD_DIM), dtype=jnp.float32)}
        return inp
    _L0_ffn_in = _L0_ffn_setup()
    _d = {'L0_attn_x': _L0_attn_in['x'], 'L0_attn_Wk': _L0_attn_in['Wk'], 'L0_attn_Wv': _L0_attn_in['Wv'], 'L0_attn_Wr': _L0_attn_in['Wr'], 'L0_attn_Wo': _L0_attn_in['Wo'], 'L0_attn_time_decay': _L0_attn_in['time_decay'], 'L0_attn_time_first': _L0_attn_in['time_first'], 'L0_attn_mixer_scale': _L0_attn_in['mixer_scale'], 'L0_attn_Wfc': _L0_attn_in['Wfc'], 'L0_attn_Wmlp': _L0_attn_in['Wmlp'], 'L0_attn_mlp_scale': _L0_attn_in['mlp_scale'], 'L0_ffn_Wq': _L0_ffn_in['Wq'], 'L0_ffn_bq': _L0_ffn_in['bq'], 'L0_ffn_Wk': _L0_ffn_in['Wk'], 'L0_ffn_bk': _L0_ffn_in['bk'], 'L0_ffn_Wv': _L0_ffn_in['Wv'], 'L0_ffn_bv': _L0_ffn_in['bv'], 'L0_ffn_Wp': _L0_ffn_in['Wp'], 'L0_ffn_bp': _L0_ffn_in['bp'], 'L0_ffn_Wr': _L0_ffn_in['Wr'], 'L0_ffn_br': _L0_ffn_in['br'], 'L0_ffn_Ws': _L0_ffn_in['Ws'], 'L0_ffn_bs': _L0_ffn_in['bs'], 'L0_ffn_temperature': _L0_ffn_in['temperature'], 'L0_ffn_query_embedding': _L0_ffn_in['query_embedding']}
    _x0 = _d['L0_attn_x']
    _d['L0_attn_x'] = jax.random.normal(jax.random.fold_in(jax.random.key(seed), 1), (4, 2048, 256), dtype=_x0.dtype)
    del _x0
    return _d

def reference(L0_attn_x, L0_attn_Wk, L0_attn_Wv, L0_attn_Wr, L0_attn_Wo, L0_attn_time_decay, L0_attn_time_first, L0_attn_mixer_scale, L0_attn_Wfc, L0_attn_Wmlp, L0_attn_mlp_scale, L0_ffn_Wq, L0_ffn_bq, L0_ffn_Wk, L0_ffn_bk, L0_ffn_Wv, L0_ffn_bv, L0_ffn_Wp, L0_ffn_bp, L0_ffn_Wr, L0_ffn_br, L0_ffn_Ws, L0_ffn_bs, L0_ffn_temperature, L0_ffn_query_embedding):

    def _L0_attn_ref(x, Wk, Wv, Wr, Wo, time_decay, time_first, mixer_scale, Wfc, Wmlp, mlp_scale):
        import jax, jax.numpy as jnp
        import numpy as np
        EPS = 1e-06

        def _rms(x):
            return x * jax.lax.rsqrt(jnp.mean(x * x, axis=-1, keepdims=True) + EPS)
        normed = _rms(x)
        k = normed @ Wk.T
        v = normed @ Wv.T
        r = jax.nn.sigmoid(normed @ Wr.T)
        ew = jnp.exp(-jnp.exp(time_decay))
        eu = jnp.exp(time_first)
        kv = (k * v).transpose(1, 0, 2)
        state0 = jnp.zeros((x.shape[0], x.shape[2]), x.dtype)

        def step(state, kvt):
            wkv = state + eu * kvt
            return (ew * state + kvt, wkv)
        _, wkv = jax.lax.scan(step, state0, kv)
        mixer_out = r * wkv.transpose(1, 0, 2) @ Wo.T
        x = x + mixer_scale[None, None, :] * mixer_out
        h = jax.nn.leaky_relu(_rms(x) @ Wfc.T, negative_slope=0.5)
        x = x + mlp_scale[None, None, :] * (h * h @ Wmlp.T)
        return x

    def _L0_ffn_ref(x, Wq, bq, Wk, bk, Wv, bv, Wp, bp, Wr, br, Ws, bs, temperature, query_embedding):
        import jax, jax.numpy as jnp
        import numpy as np
        import math
        DIM = 256
        NUM_HEADS = 16
        SHARED_HEADS = 1
        ROUTED_HEADS = 3
        HEAD_DIM = DIM // NUM_HEADS
        B, N = (2, 512)
        Bsz, Nn, C = x.shape
        H, hd = (NUM_HEADS, HEAD_DIM)

        def heads(W, b):
            y = x @ W.T + b
            return y.reshape(Bsz, Nn, H, hd).transpose(0, 2, 1, 3)
        q = heads(Wq, bq)
        k = heads(Wk, bk)
        v = heads(Wv, bv)
        q_norm = q / jnp.linalg.norm(q, axis=-1, keepdims=True)
        q_scaled = (q_norm + query_embedding[None]) * jax.nn.softplus(temperature)[None]
        attn = jnp.einsum('bhqd,bhkd->bhqk', q_scaled, k) / math.sqrt(hd)
        attn = jax.nn.softmax(attn, axis=-1)
        h = jnp.einsum('bhqk,bhkd->bhqd', attn, v)
        h = h.transpose(0, 2, 1, 3).reshape(Bsz, Nn, C)
        gates = jax.nn.softmax(h @ Wr.T + br, axis=-1)
        _, idx = jax.lax.top_k(gates, ROUTED_HEADS)
        mask = jax.nn.one_hot(idx, H - SHARED_HEADS, dtype=gates.dtype).sum(axis=-2)
        routed_gates = gates * mask * ROUTED_HEADS
        sw = jax.nn.softmax(h @ Ws.T + bs, axis=-1)
        shared_gates = sw * SHARED_HEADS
        weight_0 = sw * 2.0
        shared_gates = weight_0[..., 0:1] * shared_gates
        routed_gates = weight_0[..., 1:2] * routed_gates
        masked_gates = jnp.concatenate([shared_gates, routed_gates], axis=-1)
        out = h * masked_gates.sum(axis=-1, keepdims=True)
        return out @ Wp.T + bp
    x = L0_attn_x
    x = x + 0.5 * _L0_ffn_ref(_layernorm(x, axis=-1), L0_ffn_Wq, L0_ffn_bq, L0_ffn_Wk, L0_ffn_bk, L0_ffn_Wv, L0_ffn_bv, L0_ffn_Wp, L0_ffn_bp, L0_ffn_Wr, L0_ffn_br, L0_ffn_Ws, L0_ffn_bs, L0_ffn_temperature, L0_ffn_query_embedding)
    x = x + _L0_attn_ref(_layernorm(x, axis=-1), L0_attn_Wk, L0_attn_Wv, L0_attn_Wr, L0_attn_Wo, L0_attn_time_decay, L0_attn_time_first, L0_attn_mixer_scale, L0_attn_Wfc, L0_attn_Wmlp, L0_attn_mlp_scale)
    x = x + 0.5 * _L0_ffn_ref(_layernorm(x, axis=-1), L0_ffn_Wq, L0_ffn_bq, L0_ffn_Wk, L0_ffn_bk, L0_ffn_Wv, L0_ffn_bv, L0_ffn_Wp, L0_ffn_bp, L0_ffn_Wr, L0_ffn_br, L0_ffn_Ws, L0_ffn_bs, L0_ffn_temperature, L0_ffn_query_embedding)
    return x

_drawn_inputs = setup_inputs


def setup_inputs(seed=0):
    import zlib

    import numpy as np

    out = dict(_drawn_inputs(seed))
    spreads = {'L0_attn_mixer_scale': (1.0, 0.6),
     'L0_attn_mlp_scale': (1.0, 0.6),
     'L0_ffn_temperature': (4.151041507720947, 0.6)}
    factors = {'L0_attn_Wr': 3.364,
     'L0_attn_time_decay': 8.0,
     'L0_attn_time_first': 200.0,
     'L0_ffn_Wq': 3.449,
     'L0_ffn_bq': 8.0,
     'L0_ffn_Wk': 3.397,
     'L0_ffn_bk': 200.0,
     'L0_ffn_Wr': 8.0,
     'L0_ffn_br': 34.3,
     'L0_ffn_Ws': 8.0,
     'L0_ffn_bs': 64.0,
     'L0_ffn_query_embedding': 8.0}
    for name, (base, spread) in spreads.items():
        noise = np.random.default_rng([zlib.crc32(name.encode()), seed]).standard_normal(out[name].shape)
        drawn = base * np.exp(spread * noise) if base else spread * noise
        out[name] = jnp.asarray(drawn.astype(out[name].dtype))
    for name, factor in factors.items():
        out[name] = (out[name] * factor).astype(out[name].dtype)
    return out
```

```python
from contextlib import ExitStack

import concourse.bass as bass
from concourse import mybir

F32 = mybir.dt.float32
BF16 = mybir.dt.bfloat16
ACT = mybir.ActivationFunctionType
ALU = mybir.AluOpType
AX = mybir.AxisListType

P = 128
D = 256
KIN = D // P
H, HD = 16, 16
HPG = 4
HG = H // HPG
CH = 512
TPC = CH // P
HID = 1024
HT = HID // P
NGATE, NSH = 15, 2
TOPK = 3
LN_EPS, RMS_EPS = 1e-5, 1e-6
LEAD = 3
Q_PART = (0, 0, 1, 0, 2, 1)
K_PART = (0, 1, 0, 2, 0, 1)
NPROD = len(Q_PART)
ROWS = NPROD * HD
AUG = ROWS + 3
VSLOTS = 4
E_BANK, O_BANK, M_BANK = 0, 4, 5
M_BANKS = 3


class Steps:

    def __init__(self, sem, per_batch):
        self.sem, self.per_batch, self.n = sem, per_batch, 0

    def did(self, ins):
        ins.then_inc(self.sem, 1)
        self.n += 1
        return self.n

    def wait(self, eng, b, n=None):
        eng.wait_ge(self.sem, b * self.per_batch + (self.n if n is None else n))


def build(nc, io, B, S, totals):
    C = S // CH
    KT = S // P
    U = KT
    NC = HG * C
    assert S % CH == 0 and U > LEAD and NC > 2
    RING_PRO = 4 * (U + LEAD) + 1
    RING_BODY = 4 * U + 1
    RING_STAGE = RING_PRO + (NC - 1) * RING_BODY
    MT_PRO, MT_BODY = 4 * U + 3, 4 * (U - LEAD) + 3
    counts = {}

    with ExitStack() as ctx:
        def sb(name, shape, dt=F32):
            return ctx.enter_context(nc.sbuf_tensor(name, shape, dt))

        def sem(name):
            return ctx.enter_context(nc.semaphore(name))

        ident = sb("ident", [P, P])
        ident_bf = sb("ident_bf", [P, P], BF16)
        wq, wk, wv = (sb(n, [P, KIN, D]) for n in ("wq", "wk", "wv"))
        NOUT = D + NGATE + NSH
        wprs = sb("wprs", [P, KIN, NOUT])
        ak, av, ar, ao = (sb(n, [P, KIN, D]) for n in ("ak", "av", "ar", "ao"))
        wfc = sb("wfc", [P, KIN, HID])
        wmlp = sb("wmlp", [P, HT, D])
        bq, bv, bp = (sb(n, [P, D]) for n in ("bq", "bv", "bp"))
        embs = sb("embs", [P, D])
        brs = sb("brs", [P, NGATE + NSH])
        bk = sb("bk", [P, KIN])
        temp = sb("temp", [P, 4, H])
        mixs, mlps = sb("mixs", [P, D]), sb("mlps", [P, D])
        decay = sb("decay", [P, 2, KIN])
        mhalf = sb("mhalf", [P, 2 * H])
        x_res = sb("x_res", [P, KT, D])
        bn = sb("bn", [P, KT, 6])
        mv = sb("mv", [P, KT, 2])
        rstd = sb("rstd", [P, KT])
        msq = sb("msq", [P, KT])
        k6 = sb("k6", [P, 2 * HPG * S], BF16)
        v_ring = sb("v_ring", [P, VSLOTS, HPG, 2 * HD])
        pmax = sb("pmax", [P, HPG * TPC * C])
        negm = sb("negm", [P, 2, HPG * TPC])
        mparts = sb("mparts", [P, 3 * HPG * TPC], BF16)
        mrow = sb("mrow", [3 * HPG * TPC, P], BF16)
        rden = sb("rden", [P, KT, H])
        rnorm = sb("rnorm", [P, 2, 2, 2 * H])
        NG = NGATE + NSH
        lg = sb("lg", [P, KT, NG])
        gsm = sb("gsm", [P, 8, KT])
        sw = sb("sw", [P, KT, NSH])
        top = sb("top", [P, KT, 8])
        R = HT * CH
        work = sb("work", [P, 6 * R])
        assert KT * D <= R and HPG * S <= 2 * R

        def region(first, words=KT * D):
            return work[:, first * R:first * R + words]

        q6 = region(0, HPG * S).bitcast(BF16)
        o_t = region(2, HG * S)
        prob = region(4, 2 * HPG * CH).rearrange("p (s h q) -> p s h q", s=2, h=HPG)
        v_all = region(5).rearrange("p (t d) -> p t d", d=D)
        xn_t = region(2).rearrange("p (k t) -> p k t", k=KIN)
        xn = region(4).rearrange("p (t d) -> p t d", d=D)
        tmp = region(0, 2 * R)
        kf = tmp[:, 0:1024].rearrange("p (a t) -> p a t", a=2)
        kst = tmp[:, 1024:2560].bitcast(BF16).rearrange("p (a r t) -> p a r t", a=2, r=3)
        qn = tmp[:, 2560:3584].rearrange("p (a t) -> p a t", a=2)
        qsq = tmp[:, 3584:4608].rearrange("p (a t) -> p a t", a=2)
        qf = tmp[:, 4608:5632].rearrange("p (a t) -> p a t", a=2)
        qst = tmp[:, 5632:7168].bitcast(BF16).rearrange("p (a r t) -> p a r t", a=2, r=3)
        hn = region(0).rearrange("p (t d) -> p t d", d=D)
        h_t = region(1).rearrange("p (k t) -> p k t", k=KIN)
        y = region(4).rearrange("p (t d) -> p t d", d=D)
        n1 = region(0).rearrange("p (t d) -> p t d", d=D)
        n1_t = region(2).rearrange("p (k t) -> p k t", k=KIN)
        rw = region(3).rearrange("p (k t) -> p k t", k=KIN)
        rt = region(4).rearrange("p (k t) -> p k t", k=KIN)
        x1 = region(5).rearrange("p (t d) -> p t d", d=D)
        ksb = sb("ksb", [P, 2, CH])
        st = sb("st", [P, 2, KIN, CH + 1])
        hid = region(3, 2 * R).rearrange("p (a h t) -> p a h t", a=2, h=HT)
        z_relu = ksb

        ps = ctx.enter_context(nc.psum_tensor("ps", [P, 8, CH], F32))
        k_scr = nc.dram_tensor("k_scr", [3, D, S], BF16, kind="Internal").ap()
        q_scr = nc.dram_tensor("q_scr", [3, D, S], BF16, kind="Internal").ap()

        consts_in = sem("consts_in")
        setup_step = sem("setup_step")
        setup_done = sem("setup_done")
        pool_setup = sem("pool_setup")
        x_in = [sem(f"x_in{c}") for c in range(C)]
        x_final = sem("x_final")
        x_out = [sem(f"x_out{c}") for c in range(C)]
        dve = Steps(sem("dve_step"), totals.get("dve", 0))
        pool = Steps(sem("pool_step"), totals.get("pool", 0))
        var_ready, rstd_ready, xn_ready = sem("var_ready"), sem("rstd_ready"), sem("xn_ready")
        xt_ps, xt_sb = sem("xt_ps"), sem("xt_sb")
        q_ps, k_ps, v_ps, qt_ps = sem("q_ps"), sem("k_ps"), sem("v_ps"), sem("qt_ps")
        q_read, k_read, v_read, qt_read = sem("q_read"), sem("k_read"), sem("v_read"), sem("qt_read")
        k_stored, q_stored = ([sem(f"{x}_stored{kt}") for kt in range(KIN)] for x in "kq")
        q_sq, q_rn, q_done = sem("q_sq"), sem("q_rn"), sem("q_done")
        k_parts, q_parts = sem("k_parts"), sem("q_parts")
        ops_loaded = sem("ops_loaded")
        qk_ready, exp_done = sem("qk_ready"), sem("exp_done")
        v_slot, pv_done, o_copied = sem("v_slot"), sem("pv_done"), sem("o_copied")
        max_ready, max_free, m_step = sem("max_ready"), sem("max_free"), sem("m_step")
        mrow_ready, mrow_in = sem("mrow_ready"), sem("mrow_in")
        on_ps, hn_ready, ht_ps, ht_sb, y_ps, y_read = (
            sem(n) for n in ("on_ps", "hn_ready", "ht_ps", "ht_sb", "y_ps", "y_read"))
        gate_in, gate_exp, bp_added = sem("gate_in"), sem("gate_exp"), sem("bp_added")
        a_var, a_rstd, x1_ready, sq_done, rms_ready, n1_ready = (
            sem(n) for n in ("a_var", "a_rstd", "x1_ready", "sq_done", "rms_ready", "n1_ready"))
        nt_ps, nt_sb = sem("nt_ps"), sem("nt_sb")
        kvr_ps, k_copied, r_exp, kv_read = sem("kvr_ps"), sem("k_copied"), sem("r_exp"), sem("kv_read")
        r_den, rw_ready, mix_ps, x2_ready = sem("r_den"), sem("rw_ready"), sem("mix_ps"), sem("x2_ready")
        sq2_done, rms2_ready, n2_ready, mt_ps, mt_sb = (
            sem(n) for n in ("sq2_done", "rms2_ready", "n2_ready", "mt_ps", "mt_sb"))
        fc_relu = sem("fc_relu")
        fc_ps, fc_read, hid_ready, out_ps, out_read = (
            sem(n) for n in ("fc_ps", "fc_read", "hid_ready", "out_ps", "out_read"))
        block = ctx.enter_context(nc.Block())

        NCONST = 24

        def waited(eng):
            eng.nop(nofuse=True)

        @block.sync
        def _(sp):
            def tiles(w, n):
                return w.rearrange("(k p) n -> p k n", k=n)

            for dst, src in [
                (ident[:, :], io["ident"]),
                (wq[:, :, :], tiles(io["wq_t"], KIN)), (wk[:, :, :], tiles(io["wk_t"], KIN)),
                (wv[:, :, :], tiles(io["wv_t"], KIN)),
                (wprs[:, :, 0:D], tiles(io["wp_t"], KIN)),
                (wprs[:, :, D:D + NGATE], tiles(io["wr_t"], KIN)),
                (wprs[:, :, D + NGATE:NOUT], tiles(io["ws_t"], KIN)),
                (ak[:, :, :], tiles(io["ak_t"], KIN)), (av[:, :, :], tiles(io["av_t"], KIN)),
                (ar[:, :, :], tiles(io["ar_t"], KIN)), (ao[:, :, :], tiles(io["ao_t"], KIN)),
                (wfc[:, :, :], tiles(io["wfc_t"], KIN)), (wmlp[:, :, :], tiles(io["wmlp_t"], HT)),
                (bq[:, :], io["bq"].partition_broadcast(P)), (bv[:, :], io["bv"].partition_broadcast(P)),
                (bp[:, :], io["bp"].partition_broadcast(P)), (embs[:, :], io["emb"].partition_broadcast(P)),
                (brs[:, 0:NGATE], io["br"].partition_broadcast(P)),
                (brs[:, NGATE:NG], io["bs"].partition_broadcast(P)),
                (temp[:, 1, :], io["temp"].partition_broadcast(P)),
                (mixs[:, :], io["mix"].partition_broadcast(P)), (mlps[:, :], io["mlp"].partition_broadcast(P)),
                (bk[:, :], io["bk_cols"]),
                (decay[:, :, :], io["decay_cols"]),
            ]:
                sp.dma_start(dst, src).then_inc(consts_in, 16)

            def load_operands(s, hg):
                half = (hg % 2) * HPG * S
                for r in range(NPROD):
                    for op, scr, part in ((k6, k_scr, K_PART[r]), (q6, q_scr, Q_PART[r])):
                        sp.dma_start(
                            op[HD * r:HD * r + HD, half:half + HPG * S].rearrange("d (h t) -> d h t", h=HPG),
                            scr[part, hg * HPG * HD:(hg + 1) * HPG * HD, :].rearrange("(h d) t -> d h t", h=HPG),
                        ).then_inc(ops_loaded, 16)

            def ffn(s):
                for c in range(C):
                    for kt in range(KIN):
                        sp.wait_ge(k_parts, s * KIN * C + KIN * c + kt + 1)
                        sp.dma_start(k_scr[:, kt * P:(kt + 1) * P, c * CH:(c + 1) * CH].rearrange("r p t -> p r t"),
                                     kst[:, kt, :, :]).then_inc(k_stored[kt], 16)
                    for kt in range(KIN):
                        sp.wait_ge(q_parts, s * KIN * C + KIN * c + kt + 1)
                        sp.dma_start(q_scr[:, kt * P:(kt + 1) * P, c * CH:(c + 1) * CH].rearrange("r p t -> p r t"),
                                     qst[:, kt, :, :]).then_inc(q_stored[kt], 16)
                for stored in (*k_stored, *q_stored):
                    sp.wait_ge(stored, (s + 1) * 16 * C)
                load_operands(s, 0)
                sp.wait_ge(ops_loaded, 32 * NPROD * (s * HG + 1))
                load_operands(s, 1)

                def load_mrow(ch):
                    sp.wait_ge(mrow_ready, s * NC + ch + 1)
                    at = ((ch // C) % 2) * (HPG * S) + (ch % C) * CH
                    for r in range(3):
                        for h in range(HPG):
                            sp.dma_start(q6[ROWS + r:ROWS + r + 1, bass.ds(at + h * S, CH)]
                                         .rearrange("o (x q) -> o x q", q=P),
                                         mrow[(r * HPG + h) * TPC:(r * HPG + h + 1) * TPC, :]).then_inc(mrow_in, 16)

                load_mrow(0)
                for hg in range(HG):
                    with sp.Fori(0, C if hg < HG - 1 else C - 1) as c:
                        load_mrow(hg * C + c + 1)
                    if hg + 2 < HG:
                        sp.wait_ge(qk_ready, 2 * U * (s * NC + (hg + 1) * C))
                        sp.wait_ge(ops_loaded, 32 * NPROD * (s * HG + hg + 2))
                        load_operands(s, hg + 2)

            with sp.Fori(0, B) as b:
                xb = io["x"][bass.ds(b, 1), :, :].rearrange("o (t p) d -> p (o t) d", p=P)
                ob = io["out"][bass.ds(b, 1), :, :].rearrange("o (t p) d -> p (o t) d", p=P)
                for c in range(C):
                    sp.wait_ge(x_out[c], b * 16)
                    sp.dma_start(x_res[:, c * TPC:(c + 1) * TPC, :], xb[:, c * TPC:(c + 1) * TPC, :])\
                      .then_inc(x_in[c], 16)
                for layer in range(2):
                    ffn(b * 2 + layer)
                for c in range(C):
                    sp.wait_ge(x_final, b * C + c + 1)
                    sp.dma_start(ob[:, c * TPC:(c + 1) * TPC, :], x_res[:, c * TPC:(c + 1) * TPC, :])\
                      .then_inc(x_out[c], 16)
            for c in range(C):
                sp.wait_ge(x_out[c], B * 16)

        @block.gpsimd
        def _(gp):
            gp.memset(mhalf[:, :], -0.5).then_inc(pool_setup, 1)
            gp.wait_ge(pool_setup, 1)
            gp.memset(v_ring[:, :, :, HD:2 * HD], 1.0).then_inc(pool_setup, 1)
            gp.wait_ge(pool_setup, 2)
            gp.memset(k6[ROWS:AUG, :], 1.0).then_inc(pool_setup, 1)
            gp.wait_ge(pool_setup, 3)
            gp.wait_ge(setup_done, 1)

            def inv_sqrt(b, out, src, mul, add, n):
                pool.did(gp.tensor_scalar(out, src, mul, add, ALU.mult, ALU.add))
                pool.wait(gp, b)
                return gp.tensor_tensor(out, out, mhalf[:, 0:n], ALU.pow)

            def ffn(b, s):
                gp.wait_ge(var_ready, s + 1)
                waited(gp)
                inv_sqrt(b, rstd[:, :], mv[:, :, 1], 1.0, LN_EPS, KT).then_inc(rstd_ready, 1)
                for c in range(C):
                    for a in range(2):
                        gp.wait_ge(q_sq, s * 2 * C + 2 * c + a + 1)
                        pool.did(gp.tensor_tensor(rnorm[:, a, 1, :], rnorm[:, a, 0, :], mhalf[:, :], ALU.pow))
                        pool.wait(gp, b)
                        gp.tensor_tensor(rnorm[:, a, 0, :].rearrange("p (t h) -> p t h", h=H),
                                         rnorm[:, a, 1, :].rearrange("p (t h) -> p t h", h=H),
                                         temp[:, 0:1, :].broadcast_to([P, 2, H]), ALU.mult).then_inc(q_rn, 1)
                    for a in range(KIN):
                        gp.wait_ge(k_read, s * KIN * C + KIN * c + a + 1)
                        pool.did(gp.tensor_tensor(kf[:, a, :], kf[:, a, :], kst[:, a, 0, :], ALU.subtract))
                        pool.wait(gp, b)
                        waited(gp)
                        pool.did(gp.tensor_copy(kst[:, a, 1, :], kf[:, a, :]))
                        pool.wait(gp, b)
                        gp.tensor_tensor(kst[:, a, 2, :], kf[:, a, :], kst[:, a, 1, :], ALU.subtract)\
                          .then_inc(k_parts, 1)
                gp.wait_ge(xn_ready, (s + 1) * C)
                gp.tensor_tensor(x_res[:, :, :], x_res[:, :, :],
                                 bp[:, :].unsqueeze(1).broadcast_to([P, KT, D]), ALU.add).then_inc(bp_added, 1)
                gp.wait_ge(v_read, (s + 1) * 2 * C)
                waited(gp)

                def v_slots(ch, g0):
                    group = gp.snap((ch // C) * (HPG * HD)) if not isinstance(ch, int) else (ch // C) * HPG * HD
                    for u in range(U):
                        gp.wait_ge(pv_done, g0 + u + 1)
                        waited(gp)
                        gp.tensor_copy(v_ring[:, u % VSLOTS, :, 0:HD],
                                       v_all[:, u, bass.ds(group, HPG * HD)]
                                       .rearrange("p (h d) -> p h d", h=HPG)).then_inc(v_slot, 1)

                with gp.Fori(0, NC) as i:
                    v_slots(i, (s * NC + i) * U)

            with gp.Fori(0, B) as b:
                pool.n = 0
                ffn(b, b * 2)
                gp.wait_ge(a_var, b + 1)
                waited(gp)
                inv_sqrt(b, rstd[:, :], mv[:, :, 1], 1.0, LN_EPS, KT).then_inc(a_rstd, 1)
                gp.wait_ge(sq_done, b * KT + KT)
                waited(gp)
                inv_sqrt(b, msq[:, :], msq[:, :], 1.0 / D, RMS_EPS, KT).then_inc(rms_ready, 1)
                for c in range(C):
                    for kt in range(KIN):
                        gp.wait_ge(r_exp, b * KIN * C + KIN * c + kt + 1)
                        waited(gp)
                        r = rt[:, kt, c * CH:(c + 1) * CH]
                        gp.tensor_scalar(r, r, 1.0, None, ALU.add).then_inc(r_den, 1)
                gp.wait_ge(sq2_done, b * KT + KT)
                waited(gp)
                inv_sqrt(b, msq[:, :], msq[:, :], 1.0 / D, RMS_EPS, KT).then_inc(rms2_ready, 1)
                ffn(b, b * 2 + 1)
            counts["pool"] = pool.n

        @block.scalar
        def _(act):
            act.wait_ge(setup_step, 2)
            act.activation(temp[:, 2, :], temp[:, 2, :], ACT.Exp, scale=-1.0).then_inc(setup_step, 1)
            act.activation(decay[:, :, :], decay[:, :, :], ACT.Exp).then_inc(setup_step, 1)
            act.wait_ge(setup_step, 5)
            act.activation(temp[:, 2, :], temp[:, 2, :], ACT.Ln).then_inc(setup_step, 1)
            act.activation(decay[:, 0, :], decay[:, 0, :], ACT.Exp, scale=-1.0).then_inc(setup_step, 1)
            act.wait_ge(setup_done, 1)
            act.sem_inc(exp_done, 2)
            act.sem_inc(pv_done, VSLOTS)

            def transposed(b_c, ps_sem, sb_sem, dst, c):
                for kt in range(KIN):
                    act.wait_ge(ps_sem, b_c * KIN + kt + 1)
                    act.copy(dst[:, kt, c * CH:(c + 1) * CH], ps[:, kt, :]).then_inc(sb_sem, 1)

            def ffn(b, s):
                def parts(c, bank, kind_ps, n0, f, stage, stored, bias, done):
                    for a in range(KIN):
                        act.wait_ge(kind_ps, n0 + a + 1)
                        if c >= 1:
                            act.wait_ge(stored[a], (s * C + c) * 16)
                        act.activation(f[:, a, :], ps[:, bank + a, :], ACT.Identity,
                                       bias=bias[:, a:a + 1] if bias is not None else 0.0)
                        act.activation(stage[:, a, 0, :], ps[:, bank + a, :], ACT.Identity,
                                       bias=bias[:, a:a + 1] if bias is not None else 0.0).then_inc(done, 1)

                transposed(s * C, xt_ps, xt_sb, xn_t, 0)
                for c in range(C):
                    n0 = s * KIN * C + KIN * c
                    parts(c, 4, k_ps, n0, kf, kst, k_stored, bk, k_read)
                    if c + 1 < C:
                        transposed(s * C + c + 1, xt_ps, xt_sb, xn_t, c + 1)
                    parts(c, 0, qt_ps, n0, qf, qst, q_stored, None, qt_read)

                def chunk(i):
                    n = s * NC + i
                    for u in range(U):
                        for half in range(2):
                            act.wait_ge(qk_ready, 2 * (n * U + u) + half + 1)
                            if half == 0:
                                act.wait_ge(pv_done, n * U + u - 1 + VSLOTS)
                            act.activation(prob[:, u % 2, 2 * half:2 * half + 2, :],
                                           ps[:, E_BANK + 2 * half:E_BANK + 2 * half + 2, :], ACT.Exp)\
                               .then_inc(exp_done, 1)
                    act.wait_ge(pv_done, n * U + U + VSLOTS)
                    act.copy(o_t[:, bass.ds(i * CH, CH)], ps[:, O_BANK, :]).then_inc(o_copied, 1)

                with act.Fori(0, NC) as i:
                    chunk(i)

                for t in range(KT):
                    if t % 2 == 0:
                        p = t // 2
                        act.wait_ge(ht_ps, s * (KT // 2) + p + 1)
                        act.copy(h_t[:, :, t * P:(t + 2) * P],
                                 ps[:, 2 + p % 2, :].rearrange("p (k t) -> p k t", k=KIN)).then_inc(ht_sb, 1)
                        if p == 0:
                            continue
                    for tt in ((t - 2, t - 1) if t % 2 == 0 else ()):
                        read_y(s, tt)
                for tt in (KT - 2, KT - 1):
                    read_y(s, tt)
                act.wait_ge(gate_in, s + 1)
                act.activation(lg[:, :, :], lg[:, :, :], ACT.Exp).then_inc(gate_exp, 1)

            def read_y(s, t):
                act.wait_ge(y_ps, s * KT + t + 1)
                act.copy(y[:, t, :], ps[:, 4 + t % 4, 0:D])
                act.copy(lg[:, t, :], ps[:, 4 + t % 4, D:NOUT]).then_inc(y_read, 1)

            with act.Fori(0, B) as b:
                ffn(b, b * 2)
                for t in range(KT):
                    act.wait_ge(x1_ready, b * KT + t + 1)
                    act.activation(n1[:, t, :], x1[:, t, :], ACT.Square, accum_out=msq[:, t:t + 1])\
                       .then_inc(sq_done, 1)
                transposed(b * C, nt_ps, nt_sb, n1_t, 0)
                for c in range(C):
                    for kt in range(KIN):
                        n = b * KIN * C + KIN * c + kt
                        act.wait_ge(kvr_ps, 2 * n + 1)
                        if c >= 1:
                            act.wait_ge(kv_read, n - KIN + 1)
                        elif True:
                            act.wait_ge(kv_read, b * KIN * C)
                        act.copy(ksb[:, kt, :], ps[:, 2 + kt, :]).then_inc(k_copied, 1)
                        act.wait_ge(kvr_ps, 2 * n + 2)
                        act.activation(rt[:, kt, c * CH:(c + 1) * CH], ps[:, 6 + kt, :], ACT.Exp, scale=-1.0)\
                           .then_inc(r_exp, 1)
                    if c + 1 < C:
                        transposed(b * C + c + 1, nt_ps, nt_sb, n1_t, c + 1)
                for t in range(KT):
                    act.wait_ge(x2_ready, b * C * 2 + t // 2 + 1)
                    act.activation(n1[:, t, :], x1[:, t, :], ACT.Square, accum_out=msq[:, t:t + 1])\
                       .then_inc(sq2_done, 1)
                transposed(b * C, mt_ps, mt_sb, n1_t, 0)
                def square(n):
                    c, j = divmod(n, HT)
                    act.wait_ge(fc_read, b * HT * C + n + 1)
                    if c >= 2:
                        act.wait_ge(out_ps, b * 2 * C + 2 * (c - 1))
                    act.activation(hid[:, c % 2, j, :], z_relu[:, j % 2, :], ACT.Square, scale=0.5)\
                       .then_inc(hid_ready, 1)

                for c in range(C):
                    for j in range(HT):
                        n = HT * c + j
                        act.wait_ge(fc_ps, b * HT * C + n + 1)
                        if n >= 2:
                            act.wait_ge(hid_ready, b * HT * C + n - 1)
                        act.activation(z_relu[:, j % 2, :], ps[:, 2 + j % 4, :], ACT.Relu).then_inc(fc_relu, 1)
                        if n >= 1:
                            square(n - 1)
                    if c + 1 < C:
                        transposed(b * C + c + 1, mt_ps, mt_sb, n1_t, c + 1)
                square(HT * C - 1)
                ffn(b, b * 2 + 1)

        @block.vector
        def _(ve):
            ve.wait_ge(consts_in, 16 * NCONST)
            ve.wait_ge(pool_setup, 3)
            ve.tensor_copy(ident_bf[:, :], ident[:, :])
            ve.tensor_scalar(temp[:, 3, :], temp[:, 1, :], -1.0, None, ALU.mult).then_inc(setup_step, 1)
            ve.wait_ge(setup_step, 1)
            ve.tensor_tensor(temp[:, 2, :], temp[:, 1, :], temp[:, 3, :], ALU.max).then_inc(setup_step, 1)
            ve.tensor_tensor(ao[:, :, :], ao[:, :, :], mixs[:, :].unsqueeze(1).broadcast_to([P, KIN, D]), ALU.mult)
            ve.tensor_tensor(wmlp[:, :, :], wmlp[:, :, :], mlps[:, :].unsqueeze(1).broadcast_to([P, HT, D]), ALU.mult)
            ve.tensor_scalar(bp[:, :], bp[:, :], 0.5, None, ALU.mult)
            ve.wait_ge(setup_step, 4)
            ve.tensor_scalar(temp[:, 2, :], temp[:, 2, :], 1.0, None, ALU.add).then_inc(setup_step, 1)
            ve.wait_ge(setup_step, 7)
            ve.scalar_tensor_tensor(temp[:, 0, :], temp[:, 1, :], 0.0, temp[:, 2, :], ALU.max, ALU.add)\
              .then_inc(setup_step, 1)
            ve.wait_ge(setup_step, 8)
            ve.tensor_scalar(temp[:, 0, :], temp[:, 0, :], HD ** -0.5, None, ALU.mult).then_inc(setup_step, 1)
            ve.wait_ge(setup_step, 9)
            ve.tensor_tensor(embs[:, :].rearrange("p (h d) -> p h d", h=H), embs[:, :].rearrange("p (h d) -> p h d", h=H),
                             temp[:, 0, :].unsqueeze(2).broadcast_to([P, H, HD]), ALU.mult).then_inc(setup_step, 1)
            ve.wait_ge(setup_step, 10)
            ve.memset(st[:, :, :, 0:1], 0.0).then_inc(setup_done, 1)

            def statistics(b, src, signal, arrived=None):
                ready = []
                for t in range(KT):
                    if arrived is not None and t % TPC == 0:
                        ve.wait_ge(x_in[t // TPC], (b + 1) * 16)
                    ready.append(dve.did(ve.bn_stats(bn[:, t, :], src[:, t, :])))
                for t in range(KT):
                    dve.wait(ve, b, ready[t])
                    waited(ve)
                    ins = ve.bn_aggr(mv[:, t, :], bn[:, t, :])
                ins.then_inc(signal, 1)

            def heads(ap, t):
                return ap.rearrange("p (t h d) -> p t h d", t=t, h=H)

            def ffn(b, s, layer):
                statistics(b, x_res, var_ready, arrived=True if layer == 0 else None)
                ve.wait_ge(rstd_ready, s + 1)
                for t in range(KT):
                    ins = ve.tensor_scalar(xn[:, t, :], x_res[:, t, :], mv[:, t, 0:1], rstd[:, t:t + 1],
                                           ALU.subtract, ALU.mult)
                    if t % TPC == TPC - 1:
                        ins.then_inc(xn_ready, 1)
                for c in range(C):
                    for a in range(2):
                        n = s * 2 * C + 2 * c + a
                        ve.wait_ge(q_ps, n + 1)
                        bias = bq[:, :].unsqueeze(1).broadcast_to([P, 2, D])
                        if c >= 1:
                            ve.wait_ge(qt_ps, s * KIN * C + KIN * c)
                        k1 = dve.did(ve.tensor_tensor(qn[:, a, :].rearrange("p (t d) -> p t d", t=2),
                                                      ps[:, 2 + a, :].rearrange("p (t d) -> p t d", t=2),
                                                      bias, ALU.add))
                        dve.wait(ve, b, k1)
                        k2 = dve.did(ve.tensor_tensor(qsq[:, a, :], qn[:, a, :], qn[:, a, :], ALU.mult))
                        dve.wait(ve, b, k2)
                        ve.tensor_reduce(rnorm[:, a, 0, :].rearrange("p (t h) -> p t h", t=2),
                                         heads(qsq[:, a, :], 2), AX.X, ALU.add).then_inc(q_sq, 1)
                    for a in range(2):
                        n = s * 2 * C + 2 * c + a
                        ve.wait_ge(v_ps, n + 1)
                        ve.tensor_tensor(v_all[:, c * TPC + 2 * a:c * TPC + 2 * a + 2, :],
                                         ps[:, 6 + a, :].rearrange("p (t d) -> p t d", t=2),
                                         bv[:, :].unsqueeze(1).broadcast_to([P, 2, D]), ALU.add).then_inc(v_read, 1)
                        if a == 0:
                            pass
                    for a in range(2):
                        n = s * 2 * C + 2 * c + a
                        ve.wait_ge(q_rn, n + 1)
                        scale = rnorm[:, a, 0, :].rearrange("p (t h) -> p t h", t=2).unsqueeze(3)\
                            .broadcast_to([P, 2, H, HD])
                        k1 = dve.did(ve.tensor_tensor(heads(qn[:, a, :], 2), heads(qn[:, a, :], 2), scale, ALU.mult))
                        dve.wait(ve, b, k1)
                        v2 = qn[:, a, :].rearrange("p (t d) -> p t d", t=2)
                        ve.tensor_tensor(v2, v2, embs[:, :].unsqueeze(1).broadcast_to([P, 2, D]), ALU.add)\
                          .then_inc(q_done, 1)
                    for a in range(KIN):
                        ve.wait_ge(qt_read, s * KIN * C + KIN * c + a + 1)
                        k1 = dve.did(ve.tensor_tensor(qf[:, a, :], qf[:, a, :], qst[:, a, 0, :], ALU.subtract))
                        dve.wait(ve, b, k1)
                        k2 = dve.did(ve.tensor_copy(qst[:, a, 1, :], qf[:, a, :]))
                        dve.wait(ve, b, k2)
                        ve.tensor_tensor(qst[:, a, 2, :], qf[:, a, :], qst[:, a, 1, :], ALU.subtract)\
                          .then_inc(q_parts, 1)

                def elements(base, first, count, mt, chain, tile0):
                    tile = tile0
                    for e in range(count):
                        bank = M_BANK + e % M_BANKS
                        ve.wait_ge(max_ready, base + e + 1)
                        if e == mt:
                            ve.wait_ge(mrow_in, 16 * 3 * HPG * chain)
                            ve.tensor_copy(mrow[:, :], ps[0:3 * HPG * TPC, bank, 0:P // 2].bitcast(BF16))\
                              .then_inc(mrow_ready, 1)
                            ve.wait_ge(mrow_ready, chain + 1)
                            ve.sem_inc(max_free, 1)
                            continue
                        ve.tensor_reduce(pmax[:, tile:tile + 1], ps[:, bank, :], AX.X, ALU.max).then_inc(max_free, 1)
                        tile += 1
                        if tile == HPG * TPC * C:
                            split_max(chain, base + e + 1)
                            tile = 0

                def split_max(n, taken):
                    k = 5 * n
                    parts = mparts[:, :].rearrange("p (r x) -> p r x", r=3)
                    ve.wait_ge(max_free, taken)
                    ve.tensor_reduce(negm[:, 0, :], pmax[:, :].rearrange("p (x c) -> p x c", c=C), AX.X, ALU.max,
                                     negate=True).then_inc(m_step, 1)
                    ve.wait_ge(m_step, k + 1)
                    ve.tensor_copy(parts[:, 0, :], negm[:, 0, :]).then_inc(m_step, 1)
                    ve.wait_ge(m_step, k + 2)
                    ve.tensor_tensor(negm[:, 1, :], negm[:, 0, :], parts[:, 0, :], ALU.subtract).then_inc(m_step, 1)
                    ve.wait_ge(m_step, k + 3)
                    ve.tensor_copy(parts[:, 1, :], negm[:, 1, :]).then_inc(m_step, 1)
                    ve.wait_ge(m_step, k + 4)
                    ve.tensor_tensor(parts[:, 2, :], negm[:, 1, :], parts[:, 1, :], ALU.subtract).then_inc(m_step, 1)
                    ve.wait_ge(m_step, k + 5)

                elements(s * RING_STAGE, 0, RING_PRO, MT_PRO, s * NC, 0)
                with ve.Fori(0, NC - 1) as i:
                    elements(s * RING_STAGE + RING_PRO + i * RING_BODY, 0, RING_BODY, MT_BODY, s * NC + i + 1, 4 * LEAD)

                for t in range(KT):
                    ve.wait_ge(on_ps, s * KT + t + 1)
                    o = ps[:, t % 2, :].rearrange("p (h e) -> p h e", h=H)
                    k1 = dve.did(ve.reciprocal(rden[:, t, :].unsqueeze(2), o[:, :, HD:HD + 1]))
                    dve.wait(ve, b, k1)
                    ve.tensor_tensor(hn[:, t, :].rearrange("p (h d) -> p h d", h=H), o[:, :, 0:HD],
                                     rden[:, t, :].unsqueeze(2).broadcast_to([P, H, HD]), ALU.mult)\
                      .then_inc(hn_ready, 1)
                ve.wait_ge(y_read, (s + 1) * KT)

                def link(ins):
                    dve.did(ins)
                    dve.wait(ve, b)

                routed, shared = lg[:, :, 0:NGATE], lg[:, :, NGATE:NG]
                col = [gsm[:, j, :].unsqueeze(2) for j in range(8)]
                link(ve.tensor_tensor(lg[:, :, :], lg[:, :, :], brs[:, :].unsqueeze(1).broadcast_to([P, KT, NG]), ALU.add))
                ve.tensor_reduce(col[0], routed, AX.X, ALU.max)
                link(ve.tensor_reduce(col[1], shared, AX.X, ALU.max))
                link(ve.tensor_tensor(routed, routed, col[0].broadcast_to([P, KT, NGATE]), ALU.subtract))
                ve.tensor_tensor(shared, shared, col[1].broadcast_to([P, KT, NSH]), ALU.subtract).then_inc(gate_in, 1)
                ve.wait_ge(gate_exp, s + 1)
                link(ve.tensor_reduce(col[2], routed, AX.X, ALU.add))
                dve.did(ve.tensor_reduce(col[3], shared, AX.X, ALU.add))
                for t in range(KT):
                    last = ve.max(top[:, t, :], lg[:, t, 0:NGATE])
                link(last)
                link(ve.tensor_reduce(col[4], top[:, :, 0:TOPK], AX.X, ALU.add))
                link(ve.reciprocal(gsm[:, 2:4, :], gsm[:, 2:4, :]))
                link(ve.tensor_tensor(col[4], col[4], col[2], ALU.mult))
                link(ve.tensor_tensor(sw[:, :, :], shared, col[3].broadcast_to([P, KT, NSH]), ALU.mult))
                link(ve.tensor_tensor(col[5], sw[:, :, 0:1], sw[:, :, 1:2], ALU.add))
                link(ve.tensor_tensor(col[5], col[5], sw[:, :, 0:1], ALU.mult))
                link(ve.scalar_tensor_tensor(col[6], col[4], float(TOPK), sw[:, :, 1:2], ALU.mult, ALU.mult))
                link(ve.tensor_tensor(col[7], col[5], col[6], ALU.add))
                ve.wait_ge(bp_added, s + 1)
                for t in range(KT):
                    last = ve.scalar_tensor_tensor(x_res[:, t, :], y[:, t, :], gsm[:, 7, t:t + 1], x_res[:, t, :],
                                                   ALU.mult, ALU.add)
                    if layer == 1 and t % TPC == TPC - 1:
                        last.then_inc(x_final, 1)
                if layer == 0:
                    link(last)

            def recurrence(b):
                statistics(b, x_res, a_var)
                ve.wait_ge(a_rstd, b + 1)
                for t in range(KT):
                    ve.tensor_scalar(x1[:, t, :], x_res[:, t, :], mv[:, t, 0:1], rstd[:, t:t + 1],
                                     ALU.subtract, ALU.mult).then_inc(x1_ready, 1)
                ve.wait_ge(rms_ready, b + 1)
                for t in range(KT):
                    last = ve.tensor_scalar(n1[:, t, :], x1[:, t, :], msq[:, t:t + 1], None, ALU.mult)
                    if t % TPC == TPC - 1:
                        last.then_inc(n1_ready, 1)

                def add_mix(c):
                    for a in range(2):
                        ve.wait_ge(mix_ps, b * 2 * C + 2 * c + a + 1)
                        x = x1[:, c * TPC + 2 * a:c * TPC + 2 * a + 2, :]
                        ve.tensor_tensor(x, x, ps[:, a, :].rearrange("p (t d) -> p t d", t=2), ALU.add)\
                          .then_inc(x2_ready, 1)

                for c in range(C):
                    span = slice(c * CH, (c + 1) * CH)
                    kv = [rw[:, kt, span] for kt in range(KIN)]
                    for kt in range(KIN):
                        n = b * KIN * C + KIN * c + kt
                        ve.wait_ge(k_copied, n + 1)
                        dve.did(ve.tensor_tensor(kv[kt], ps[:, 4 + kt, :], ksb[:, kt, :], ALU.mult))
                        dve.wait(ve, b)
                        if c >= 1:
                            dve.did(ve.tensor_copy(st[:, c % 2, kt, 0:1], st[:, (c - 1) % 2, kt, CH:CH + 1]))
                        else:
                            dve.did(ve.memset(st[:, 0, kt, 0:1], 0.0))
                        dve.wait(ve, b)
                        dve.did(ve.tensor_tensor_scan(st[:, c % 2, kt, 1:CH + 1],
                                                      decay[:, 0, kt:kt + 1].broadcast_to([P, CH]), kv[kt],
                                                      st[:, c % 2, kt, 0:1], ALU.mult, ALU.add))
                        dve.wait(ve, b)
                        ve.scalar_tensor_tensor(kv[kt], kv[kt], decay[:, 1, kt:kt + 1], st[:, c % 2, kt, 0:CH],
                                                ALU.mult, ALU.add).then_inc(kv_read, 1)
                    for kt in range(KIN):
                        n = b * KIN * C + KIN * c + kt
                        ve.wait_ge(r_den, n + 1)
                        dve.did(ve.reciprocal(rt[:, kt, span], rt[:, kt, span]))
                        dve.wait(ve, b)
                        ve.wait_ge(kv_read, n + 1)
                        ve.tensor_tensor(kv[kt], kv[kt], rt[:, kt, span], ALU.mult).then_inc(rw_ready, 1)
                    if c >= 1:
                        add_mix(c - 1)
                add_mix(C - 1)
                ve.wait_ge(rms2_ready, b + 1)
                for t in range(KT):
                    last = ve.tensor_scalar(n1[:, t, :], x1[:, t, :], msq[:, t:t + 1], None, ALU.mult)
                    if t % TPC == TPC - 1:
                        last.then_inc(n2_ready, 1)
                for c in range(C):
                    xs = x_res[:, c * TPC:(c + 1) * TPC, :]
                    dve.did(ve.tensor_tensor(xs, xs, x1[:, c * TPC:(c + 1) * TPC, :], ALU.add))
                def add_out(c):
                    for a in range(2):
                        ve.wait_ge(out_ps, b * 2 * C + 2 * c + a + 1)
                        x = x_res[:, c * TPC + 2 * a:c * TPC + 2 * a + 2, :]
                        dve.wait(ve, b)
                        ve.tensor_tensor(x, x, ps[:, 6 + a, :].rearrange("p (t d) -> p t d", t=2), ALU.add)\
                          .then_inc(out_read, 1)

                for c in range(C):
                    for j in range(HT):
                        ve.wait_ge(fc_relu, b * HT * C + HT * c + j + 1)
                        ve.tensor_tensor(z_relu[:, j % 2, :], z_relu[:, j % 2, :], ps[:, 2 + j % 4, :], ALU.add)\
                          .then_inc(fc_read, 1)
                    if c >= 1:
                        add_out(c - 1)
                add_out(C - 1)
                ve.wait_ge(out_read, (b + 1) * 2 * C)

            with ve.Fori(0, B) as b:
                dve.n = 0
                ffn(b, b * 2, 0)
                recurrence(b)
                ffn(b, b * 2 + 1, 1)
            counts["dve"] = dve.n

        @block.tensor
        def _(pe):
            pe.wait_ge(setup_done, 1)

            def transposes(c, src, ready, ready_at, signal, banks=(0, 1)):
                pe.wait_ge(ready, ready_at)
                for kt in range(KIN):
                    for j in range(TPC):
                        last = pe.transpose(ps[:, banks[kt], j * P:(j + 1) * P],
                                            src[:, c * TPC + j, kt * P:(kt + 1) * P], ident[:, :])
                    last.then_inc(signal, 1)

            def natural(c, a, w, acts, bank, signal):
                for j in range(2):
                    t = c * TPC + 2 * a + j
                    for kt in range(KIN):
                        last = pe.matmul(ps[:, bank, j * D:(j + 1) * D], acts[:, kt, t * P:(t + 1) * P], w[:, kt, :],
                                         start=kt == 0, stop=kt == KIN - 1)
                last.then_inc(signal, 1)

            def columns(c, m, w, acts, bank):
                for kt in range(KIN):
                    last = pe.matmul(ps[:, bank, :], w[:, kt, m * P:(m + 1) * P], acts[:, kt, c * CH:(c + 1) * CH],
                                     start=kt == 0, stop=kt == KIN - 1)
                return last

            def ffn(s):
                transposes(0, xn, xn_ready, s * C + 1, xt_ps)
                for c in range(C):
                    n = s * 2 * C + 2 * c
                    pe.wait_ge(xt_sb, n + 2)
                    for a in range(2):
                        if c >= 1:
                            pe.wait_ge(q_sq, n - 2 + a + 1)
                        natural(c, a, wq, xn_t, 2 + a, q_ps)
                    for a in range(KIN):
                        if c >= 1:
                            pe.wait_ge(k_read, n - 2 + a + 1)
                        columns(c, a, wk, xn_t, 4 + a).then_inc(k_ps, 1)
                    for a in range(2):
                        if c >= 1:
                            pe.wait_ge(v_read, n - 2 + a + 1)
                        natural(c, a, wv, xn_t, 6 + a, v_ps)
                    if c + 1 < C:
                        if c >= 1:
                            pe.wait_ge(qt_read, n)
                        transposes(c + 1, xn, xn_ready, s * C + c + 2, xt_ps)
                        pe.wait_ge(xt_sb, n + 4)
                    pe.wait_ge(q_done, n + 2)
                    for kt in range(KIN):
                        for j in range(TPC):
                            a, t = divmod(j, 2)
                            last = pe.transpose(ps[:, kt, j * P:(j + 1) * P],
                                                qn[:, a, t * D + kt * P:t * D + (kt + 1) * P], ident[:, :])
                        last.then_inc(qt_ps, 1)

                n = (s + 1) * 2 * C
                for sm in (qt_read, k_read, v_read):
                    pe.wait_ge(sm, n)

                def offsets(ch):
                    at_k = ((ch // C) % 2) * (HPG * S)
                    at_q = at_k + (ch % C) * CH
                    return (at_k, at_q) if isinstance(ch, int) else (pe.snap(at_k), pe.snap(at_q))

                def scores(at, u, half, n):
                    pe.wait_ge(exp_done, 2 * (n * U + u) + half + 1)
                    for h in (2 * half, 2 * half + 1):
                        last = pe.matmul(ps[:, E_BANK + h, :], k6[0:AUG, bass.ds(at[0] + h * S + u * P, P)],
                                         q6[0:AUG, bass.ds(at[1] + h * S, CH)], start=True, stop=True)
                    last.then_inc(qk_ready, 1)

                def element(base, e, mt, m_at, at, tile):
                    back = e - M_BANKS + 1 if e >= M_BANKS else (-1, 0, -2)[e]
                    if not (mt == MT_PRO and e < M_BANKS):
                        pe.wait_ge(max_free, base + back)
                    bank = M_BANK + e % M_BANKS
                    if e == mt:
                        pe.wait_ge(m_step, 5 * m_at + 5)
                        waited(pe)
                        pe.transpose(ps[0:3 * HPG * TPC, bank, 0:P // 2].bitcast(BF16), mparts[:, :], ident_bf[:, :])\
                          .then_inc(max_ready, 1)
                        return
                    x, kc = divmod(tile, C)
                    h, qt = divmod(x, TPC)
                    pe.matmul(ps[:, bank, :], q6[0:ROWS, bass.ds(at[1] + h * S + qt * P, P)],
                              k6[0:ROWS, bass.ds(at[0] + h * S + kc * CH, CH)], start=True, stop=True)\
                      .then_inc(max_ready, 1)

                def products(u, n):
                    pe.wait_ge(exp_done, 2 * (n * U + u) + 4)
                    pe.wait_ge(v_slot, n * U + u + 1)
                    if u == 0:
                        pe.wait_ge(o_copied, n)
                    for h in range(HPG):
                        last = pe.matmul(ps[32 * h:32 * h + 2 * HD, O_BANK, :], v_ring[:, u % VSLOTS, h, :],
                                         prob[:, u % 2, h, :], start=u == 0, stop=u == U - 1)
                    last.then_inc(pv_done, 1)

                NT = HPG * TPC * C
                pe.wait_ge(ops_loaded, 32 * NPROD * (s * HG + 1))
                at0, at1 = offsets(0), offsets(1)
                tile = 0
                for e in range(RING_PRO):
                    first = e < NT
                    if e == NT and 1 // C > 0:
                        pe.wait_ge(ops_loaded, 32 * NPROD * (s * HG + 2))
                    element(s * RING_STAGE, e, MT_PRO, s * NC, at0 if first else at1, tile % NT)
                    tile += e != MT_PRO
                pe.wait_ge(mrow_in, 16 * 3 * HPG * (s * NC + 1))
                for half in range(2):
                    scores(at0, 0, half, s * NC)

                with pe.Fori(0, NC - 1) as i:
                    n = s * NC + i
                    here, ahead, ahead2 = offsets(i), offsets(i + 1), offsets((i + 2) % NC)
                    base = s * RING_STAGE + RING_PRO + i * RING_BODY
                    tile, e = 4 * LEAD, 0
                    for u in range(U):
                        if u == U - 1:
                            pe.wait_ge(mrow_in, 16 * 3 * HPG * (n + 2))
                        for half in range(2):
                            if u < U - 1:
                                scores(here, u + 1, half, n)
                            else:
                                scores(ahead, 0, half, n + 1)
                            for _ in range(2 + (u == U - 1 and half == 1)):
                                if tile == NT:
                                    pe.wait_ge(ops_loaded, 32 * NPROD * (s * HG + ((i + 2) % NC) // C + 1))
                                element(base, e, MT_BODY, n + 1, ahead if tile < NT else ahead2, tile % NT)
                                tile += e != MT_BODY
                                e += 1
                        products(u, n)
                n = s * NC + NC - 1
                at = offsets(NC - 1)
                for u in range(U):
                    if u < U - 1:
                        for half in range(2):
                            scores(at, u + 1, half, n)
                    products(u, n)

                pe.wait_ge(o_copied, (s + 1) * NC)
                pe.wait_ge(max_free, (s + 1) * RING_STAGE)

                def turn(t):
                    if t >= 2:
                        pe.wait_ge(hn_ready, s * KT + t - 1)
                    for hg in range(HG):
                        last = pe.transpose(ps[:, t % 2, hg * P:(hg + 1) * P], o_t[:, hg * S + t * P:hg * S + (t + 1) * P],
                                            ident[:, :])
                    last.then_inc(on_ps, 1)

                def back(p):
                    pe.wait_ge(hn_ready, s * KT + 2 * p + 2)
                    if p >= 2:
                        pe.wait_ge(ht_sb, s * (KT // 2) + p - 1)
                    for j in range(2):
                        for kt in range(KIN):
                            last = pe.transpose(ps[:, 2 + p % 2, kt * 2 * P + j * P:kt * 2 * P + (j + 1) * P],
                                                hn[:, 2 * p + j, kt * P:(kt + 1) * P], ident[:, :])
                    last.then_inc(ht_ps, 1)

                def project(t):
                    pe.wait_ge(ht_sb, s * (KT // 2) + t // 2 + 1)
                    if t >= 4:
                        pe.wait_ge(y_read, s * KT + t - 3)
                    for kt in range(KIN):
                        last = pe.matmul(ps[:, 4 + t % 4, 0:NOUT], h_t[:, kt, t * P:(t + 1) * P], wprs[:, kt, :],
                                         start=kt == 0, stop=kt == KIN - 1)
                    last.then_inc(y_ps, 1)

                turn(0)
                turn(1)
                for p in range(KT // 2):
                    if 2 * p + 2 < KT:
                        turn(2 * p + 2)
                        turn(2 * p + 3)
                    back(p)
                    if p >= 1:
                        project(2 * p - 2)
                        project(2 * p - 1)
                project(KT - 2)
                project(KT - 1)
                pe.wait_ge(y_read, (s + 1) * KT)

            def recurrence(b):
                transposes(0, n1, n1_ready, b * C + 1, nt_ps)

                def mix(c):
                    pe.wait_ge(rw_ready, b * KIN * C + KIN * (c + 1))
                    if c + 2 < C:
                        pe.wait_ge(nt_sb, b * KIN * C + KIN * (c + 3))
                    else:
                        pe.wait_ge(nt_sb, (b + 1) * KIN * C)
                    for a in range(2):
                        if c >= 1:
                            pe.wait_ge(x2_ready, b * 2 * C + 2 * (c - 1) + a + 1)
                        natural(c, a, ao, rw, a, mix_ps)

                for c in range(C):
                    n = b * KIN * C + KIN * c
                    pe.wait_ge(nt_sb, n + KIN)
                    for kt in range(KIN):
                        if c >= 1:
                            pe.wait_ge(kv_read, n - KIN + kt + 1)
                            pe.wait_ge(r_exp, n - KIN + kt + 1)
                        columns(c, kt, ak, n1_t, 2 + kt)
                        columns(c, kt, av, n1_t, 4 + kt).then_inc(kvr_ps, 1)
                        columns(c, kt, ar, n1_t, 6 + kt).then_inc(kvr_ps, 1)
                    if c + 1 < C:
                        if c >= 2:
                            pe.wait_ge(x2_ready, b * 2 * C + 2 * (c - 1))
                        transposes(c + 1, n1, n1_ready, b * C + c + 2, nt_ps)
                    if c >= 1:
                        mix(c - 1)
                mix(C - 1)
                pe.wait_ge(x2_ready, (b + 1) * 2 * C)
                transposes(0, n1, n2_ready, b * C + 1, mt_ps)

                def down(c):
                    pe.wait_ge(hid_ready, b * HT * C + HT * (c + 1))
                    for a in range(2):
                        if c >= 1:
                            pe.wait_ge(out_read, b * 2 * C + 2 * (c - 1) + a + 1)
                        for j in range(2):
                            t = 2 * a + j
                            for m in range(HT):
                                last = pe.matmul(ps[:, 6 + a, j * D:(j + 1) * D], hid[:, c % 2, m, t * P:(t + 1) * P],
                                                 wmlp[:, m, :], start=m == 0, stop=m == HT - 1)
                        last.then_inc(out_ps, 1)

                for c in range(C):
                    pe.wait_ge(mt_sb, b * KIN * C + KIN * (c + 1))
                    for m in range(HT):
                        n = HT * c + m
                        if n >= 4:
                            pe.wait_ge(fc_read, b * HT * C + n - 3)
                        columns(c, m, wfc, n1_t, 2 + m % 4).then_inc(fc_ps, 1)
                    if c + 1 < C:
                        transposes(c + 1, n1, n2_ready, b * C + c + 2, mt_ps)
                    if c >= 1:
                        down(c - 1)
                down(C - 1)
                pe.wait_ge(out_read, (b + 1) * 2 * C)

            with pe.Fori(0, B) as b:
                ffn(b * 2)
                recurrence(b)
                ffn(b * 2 + 1)
    return counts


def kernel(**inputs):
    import numpy as np
    import concourse.bacc as bacc
    from concourse import mybir as _mybir
    from concourse.bass_utils import run_bass_kernel_spmd as _run

    def arr(name):
        return np.asarray(inputs[name])

    def turned(name):
        return np.ascontiguousarray(arr(name).T)

    def columns_of(*names):
        return np.ascontiguousarray(np.stack([arr(n).reshape(2, 128).T for n in names], axis=1))

    host = {
        "x": np.ascontiguousarray(arr("L0_attn_x")),
        "ident": np.eye(128, dtype=np.float32),
        "wq_t": turned("L0_ffn_Wq"), "wk_t": turned("L0_ffn_Wk"), "wv_t": turned("L0_ffn_Wv"),
        "wp_t": turned("L0_ffn_Wp"), "wr_t": turned("L0_ffn_Wr"), "ws_t": turned("L0_ffn_Ws"),
        "ak_t": turned("L0_attn_Wk"), "av_t": turned("L0_attn_Wv"), "ar_t": turned("L0_attn_Wr"),
        "ao_t": turned("L0_attn_Wo"), "wfc_t": turned("L0_attn_Wfc"), "wmlp_t": turned("L0_attn_Wmlp"),
        "bq": arr("L0_ffn_bq"), "bv": arr("L0_ffn_bv"), "bp": arr("L0_ffn_bp"),
        "br": arr("L0_ffn_br"), "bs": arr("L0_ffn_bs"),
        "emb": np.ascontiguousarray(arr("L0_ffn_query_embedding").reshape(-1)),
        "temp": np.ascontiguousarray(arr("L0_ffn_temperature").reshape(-1)),
        "mix": arr("L0_attn_mixer_scale"), "mlp": arr("L0_attn_mlp_scale"),
        "bk_cols": np.ascontiguousarray(arr("L0_ffn_bk").reshape(2, 128).T),
        "decay_cols": columns_of("L0_attn_time_decay", "L0_attn_time_first"),
    }
    B, S, _ = host["x"].shape

    def program(totals):
        nc = bacc.Bacc("TRN2", target_bir_lowering=False, num_devices=1)
        io = {n: nc.dram_tensor(f"in_{n}", a.shape, _mybir.dt.from_np(a.dtype), kind="ExternalInput").ap()
              for n, a in host.items()}
        io["out"] = nc.dram_tensor("out_0", host["x"].shape, _mybir.dt.float32, kind="ExternalOutput").ap()
        return nc, build(nc, io, B, S, totals)

    _, totals = program({})
    nc, again = program(totals)
    assert again == totals
    r = _run(nc, [{f"in_{n}": a for n, a in host.items()}], core_ids=[0])
    return r.results[0]["out_0"]
```

```python
from contextlib import ExitStack

import concourse.bass as bass
from concourse import mybir

F32 = mybir.dt.float32
BF16 = mybir.dt.bfloat16
ACT = mybir.ActivationFunctionType
ALU = mybir.AluOpType
AX = mybir.AxisListType

P = 128
D = 256
KIN = D // P
H, HD = 16, 16
HPG = 4
HG = H // HPG
CH = 512
TPC = CH // P
HID = 1024
HT = HID // P
NGATE, NSH = 15, 2
TOPK = 3
LN_EPS, RMS_EPS = 1e-5, 1e-6
LEAD = 5
MT_LAG = 7
Q_PART = (0, 0, 1, 0, 2, 1)
K_PART = (0, 1, 0, 2, 0, 1)
NPROD = len(Q_PART)
ROWS = NPROD * HD
AUG = ROWS + 3
VSLOTS = 4
E_BANK, O_BANK, M_BANK = 0, 4, 5
M_BANKS = 3


class Steps:

    def __init__(self, sem, per_batch):
        self.sem, self.per_batch, self.n = sem, per_batch, 0

    def did(self, ins):
        ins.then_inc(self.sem, 1)
        self.n += 1
        return self.n

    def wait(self, eng, b, n=None):
        eng.wait_ge(self.sem, b * self.per_batch + (self.n if n is None else n))


def build(nc, io, B, S, totals):
    C = S // CH
    KT = S // P
    U = KT
    NC = HG * C
    assert S % CH == 0 and U > LEAD and NC > 2
    RING_PRO = 4 * (U + LEAD) + 1
    RING_BODY = 4 * U + 1
    RING_STAGE = RING_PRO + (NC - 1) * RING_BODY
    RING_TURN = (RING_BODY - RING_PRO) % M_BANKS
    MT_PRO, MT_BODY = 4 * U + MT_LAG, 4 * (U - LEAD) + MT_LAG
    counts = {}

    with ExitStack() as ctx:
        def sb(name, shape, dt=F32):
            return ctx.enter_context(nc.sbuf_tensor(name, shape, dt))

        def sem(name):
            return ctx.enter_context(nc.semaphore(name))

        ident = sb("ident", [P, P])
        ident_bf = sb("ident_bf", [P, P], BF16)
        wq, wk, wv = (sb(n, [P, KIN, D]) for n in ("wq", "wk", "wv"))
        NOUT = D + NGATE + NSH
        wprs = sb("wprs", [P, KIN, NOUT])
        ak, av, ar, ao = (sb(n, [P, KIN, D]) for n in ("ak", "av", "ar", "ao"))
        wfc = sb("wfc", [P, KIN, HID])
        wmlp = sb("wmlp", [P, HT, D])
        bq, bv, bp = (sb(n, [P, D]) for n in ("bq", "bv", "bp"))
        embs = sb("embs", [P, D])
        brs = sb("brs", [P, NGATE + NSH])
        bk = sb("bk", [P, KIN])
        temp = sb("temp", [P, 4, H])
        mixs, mlps = sb("mixs", [P, D]), sb("mlps", [P, D])
        decay = sb("decay", [P, 2, KIN])
        x_res = sb("x_res", [P, KT, D])
        bn = sb("bn", [P, KT, 6])
        mv = sb("mv", [P, KT, 2])
        rstd = sb("rstd", [P, KT])
        msq = sb("msq", [P, 2, KT])
        k6 = sb("k6", [P, 2 * HPG * S], BF16)
        v_ring = sb("v_ring", [P, VSLOTS, HPG, 2 * HD])
        pmax = sb("pmax", [P, HPG * TPC * C])
        negm = sb("negm", [P, 2, HPG * TPC])
        mparts = sb("mparts", [P, 3 * HPG * TPC], BF16)
        mrow = sb("mrow", [3 * HPG, CH], BF16)
        rden = sb("rden", [P, KT, H])
        rnorm = sb("rnorm", [P, 2, TPC * H])
        newton = sb("newton", [P, TPC * H])
        NG = NGATE + NSH
        lg = sb("lg", [P, KT, NG])
        gsm = sb("gsm", [P, 8, KT])
        sw = sb("sw", [P, KT, NSH])
        top = sb("top", [P, KT, 8])
        R = HT * CH
        work = sb("work", [P, 6 * R])
        assert KT * D <= R and HPG * S <= 2 * R

        def region(first, words=KT * D):
            return work[:, first * R:first * R + words]

        q6 = region(0, HPG * S).bitcast(BF16)
        o_t = region(2, HG * S)
        prob = region(4, 2 * HPG * CH).rearrange("p (s h q) -> p s h q", s=2, h=HPG)
        v_all = region(5).rearrange("p (t d) -> p t d", d=D)
        xn_t = region(2).rearrange("p (k t) -> p k t", k=KIN)
        xn = region(4).rearrange("p (t d) -> p t d", d=D)
        tmp = region(0, 2 * R)
        kf = tmp[:, 0:1024].rearrange("p (a t) -> p a t", a=2)
        kst = tmp[:, 1024:2560].bitcast(BF16).rearrange("p (a r t) -> p a r t", a=2, r=3)
        qn = tmp[:, 2560:3584].rearrange("p (a t) -> p a t", a=2)
        qsq = tmp[:, 3584:4608].rearrange("p (a t) -> p a t", a=2)
        qf = tmp[:, 4608:5632].rearrange("p (a t) -> p a t", a=2)
        qst = tmp[:, 5632:7168].bitcast(BF16).rearrange("p (a r t) -> p a r t", a=2, r=3)
        hn = region(0).rearrange("p (t d) -> p t d", d=D)
        h_t = region(1).rearrange("p (k t) -> p k t", k=KIN)
        y = region(4).rearrange("p (t d) -> p t d", d=D)
        n1 = region(0).rearrange("p (t d) -> p t d", d=D)
        n1_t = region(2).rearrange("p (k t) -> p k t", k=KIN)
        rw = region(3).rearrange("p (k t) -> p k t", k=KIN)
        rt = region(4).rearrange("p (k t) -> p k t", k=KIN)
        x1 = region(5).rearrange("p (t d) -> p t d", d=D)
        ksb = sb("ksb", [P, 2, CH])
        st = sb("st", [P, 2, KIN, CH + 1])
        hid = region(3, 2 * R).rearrange("p (a h t) -> p a h t", a=2, h=HT)
        z_relu = ksb

        ps = ctx.enter_context(nc.psum_tensor("ps", [P, 8, CH], F32))
        k_scr = nc.dram_tensor("k_scr", [3, D, S], BF16, kind="Internal").ap()
        q_scr = nc.dram_tensor("q_scr", [3, D, S], BF16, kind="Internal").ap()

        consts_in = sem("consts_in")
        setup_step = sem("setup_step")
        setup_done = sem("setup_done")
        pool_setup = sem("pool_setup")
        x_in = [sem(f"x_in{c}") for c in range(C)]
        x_final = sem("x_final")
        x_out = [sem(f"x_out{c}") for c in range(C)]
        dve = Steps(sem("dve_step"), totals.get("dve", 0))
        pool = Steps(sem("pool_step"), totals.get("pool", 0))
        act_steps = Steps(sem("act_step"), totals.get("act", 0))
        var_ready, rstd_ready, xn_ready = sem("var_ready"), sem("rstd_ready"), sem("xn_ready")
        xt_ps, xt_sb = sem("xt_ps"), sem("xt_sb")
        q_ps, k_ps, v_ps, qt_ps = sem("q_ps"), sem("k_ps"), sem("v_ps"), sem("qt_ps")
        q_read, k_read, v_read, qt_read = sem("q_read"), sem("k_read"), sem("v_read"), sem("qt_read")
        k_stored, q_stored = ([sem(f"{x}_stored{kt}") for kt in range(KIN)] for x in "kq")
        q_added, q_ss, ms_ready = sem("q_added"), sem("q_ss"), sem("ms_ready")
        q_sq, q_rn, q_done = sem("q_sq"), sem("q_rn"), sem("q_done")
        k_parts, q_parts = sem("k_parts"), sem("q_parts")
        ops_loaded = sem("ops_loaded")
        qk_ready, exp_done = sem("qk_ready"), sem("exp_done")
        v_slot, pv_done, o_copied = sem("v_slot"), sem("pv_done"), sem("o_copied")
        max_ready, max_free, m_step = sem("max_ready"), sem("max_free"), sem("m_step")
        mrow_ready, mrow_in = sem("mrow_ready"), sem("mrow_in")
        on_ps, hn_ready, ht_ps, ht_sb, y_ps, y_read = (
            sem(n) for n in ("on_ps", "hn_ready", "ht_ps", "ht_sb", "y_ps", "y_read"))
        gate_in, gate_exp, bp_added = sem("gate_in"), sem("gate_exp"), sem("bp_added")
        a_var, a_rstd, x1_ready, sq_done, rms_ready, n1_ready = (
            sem(n) for n in ("a_var", "a_rstd", "x1_ready", "sq_done", "rms_ready", "n1_ready"))
        nt_ps, nt_sb = sem("nt_ps"), sem("nt_sb")
        kvr_ps, k_copied, r_exp, kv_read = sem("kvr_ps"), sem("k_copied"), sem("r_exp"), sem("kv_read")
        r_den, rw_ready, mix_ps, x2_ready = sem("r_den"), sem("rw_ready"), sem("mix_ps"), sem("x2_ready")
        sq2_done, rms2_ready, n2_ready, mt_ps, mt_sb = (
            sem(n) for n in ("sq2_done", "rms2_ready", "n2_ready", "mt_ps", "mt_sb"))
        fc_relu = sem("fc_relu")
        fc_ps, fc_read, hid_ready, out_ps, out_read = (
            sem(n) for n in ("fc_ps", "fc_read", "hid_ready", "out_ps", "out_read"))
        block = ctx.enter_context(nc.Block())

        NCONST = 24

        def waited(eng):
            eng.nop(nofuse=True)

        @block.sync
        def _(sp):
            def tiles(w, n):
                return w.rearrange("(k p) n -> p k n", k=n)

            for dst, src in [
                (ident[:, :], io["ident"]),
                (wq[:, :, :], tiles(io["wq_t"], KIN)), (wk[:, :, :], tiles(io["wk_t"], KIN)),
                (wv[:, :, :], tiles(io["wv_t"], KIN)),
                (wprs[:, :, 0:D], tiles(io["wp_t"], KIN)),
                (wprs[:, :, D:D + NGATE], tiles(io["wr_t"], KIN)),
                (wprs[:, :, D + NGATE:NOUT], tiles(io["ws_t"], KIN)),
                (ak[:, :, :], tiles(io["ak_t"], KIN)), (av[:, :, :], tiles(io["av_t"], KIN)),
                (ar[:, :, :], tiles(io["ar_t"], KIN)), (ao[:, :, :], tiles(io["ao_t"], KIN)),
                (wfc[:, :, :], tiles(io["wfc_t"], KIN)), (wmlp[:, :, :], tiles(io["wmlp_t"], HT)),
                (bq[:, :], io["bq"].partition_broadcast(P)), (bv[:, :], io["bv"].partition_broadcast(P)),
                (bp[:, :], io["bp"].partition_broadcast(P)), (embs[:, :], io["emb"].partition_broadcast(P)),
                (brs[:, 0:NGATE], io["br"].partition_broadcast(P)),
                (brs[:, NGATE:NG], io["bs"].partition_broadcast(P)),
                (temp[:, 1, :], io["temp"].partition_broadcast(P)),
                (mixs[:, :], io["mix"].partition_broadcast(P)), (mlps[:, :], io["mlp"].partition_broadcast(P)),
                (bk[:, :], io["bk_cols"]),
                (decay[:, :, :], io["decay_cols"]),
            ]:
                sp.dma_start(dst, src).then_inc(consts_in, 16)

            def load_operands(s, hg):
                half = (hg % 2) * HPG * S
                for r in range(NPROD):
                    for op, scr, part in ((k6, k_scr, K_PART[r]), (q6, q_scr, Q_PART[r])):
                        sp.dma_start(
                            op[HD * r:HD * r + HD, half:half + HPG * S].rearrange("d (h t) -> d h t", h=HPG),
                            scr[part, hg * HPG * HD:(hg + 1) * HPG * HD, :].rearrange("(h d) t -> d h t", h=HPG),
                        ).then_inc(ops_loaded, 16)

            def ffn(s):
                for c in range(C):
                    for kt in range(KIN):
                        sp.wait_ge(k_parts, s * KIN * C + KIN * c + kt + 1)
                        sp.dma_start(k_scr[:, kt * P:(kt + 1) * P, c * CH:(c + 1) * CH].rearrange("r p t -> p r t"),
                                     kst[:, kt, :, :]).then_inc(k_stored[kt], 16)
                    for kt in range(KIN):
                        sp.wait_ge(q_parts, s * KIN * C + KIN * c + kt + 1)
                        sp.dma_start(q_scr[:, kt * P:(kt + 1) * P, c * CH:(c + 1) * CH].rearrange("r p t -> p r t"),
                                     qst[:, kt, :, :]).then_inc(q_stored[kt], 16)
                for stored in (*k_stored, *q_stored):
                    sp.wait_ge(stored, (s + 1) * 16 * C)
                load_operands(s, 0)
                sp.wait_ge(ops_loaded, 32 * NPROD * (s * HG + 1))
                load_operands(s, 1)

                def load_mrow(ch):
                    sp.wait_ge(mrow_ready, s * NC + ch + 1)
                    rows = q6[ROWS:AUG, :].rearrange("r (g t) -> r g t", t=S)
                    sp.dma_start(rows[:, bass.ds(((ch // C) % 2) * HPG, HPG), bass.ds((ch % C) * CH, CH)],
                                 mrow[:, :]).then_inc(mrow_in, 16)

                load_mrow(0)
                for hg in range(HG):
                    with sp.Fori(0, C if hg < HG - 1 else C - 1) as c:
                        load_mrow(hg * C + c + 1)
                    if hg + 2 < HG:
                        sp.wait_ge(qk_ready, 2 * U * (s * NC + (hg + 1) * C))
                        sp.wait_ge(ops_loaded, 32 * NPROD * (s * HG + hg + 2))
                        load_operands(s, hg + 2)

            with sp.Fori(0, B) as b:
                xb = io["x"][bass.ds(b, 1), :, :].rearrange("o (t p) d -> p (o t) d", p=P)
                ob = io["out"][bass.ds(b, 1), :, :].rearrange("o (t p) d -> p (o t) d", p=P)
                for c in range(C):
                    sp.wait_ge(x_out[c], b * 16)
                    sp.dma_start(x_res[:, c * TPC:(c + 1) * TPC, :], xb[:, c * TPC:(c + 1) * TPC, :])\
                      .then_inc(x_in[c], 16)
                for layer in range(2):
                    ffn(b * 2 + layer)
                for c in range(C):
                    sp.wait_ge(x_final, b * C + c + 1)
                    sp.dma_start(ob[:, c * TPC:(c + 1) * TPC, :], x_res[:, c * TPC:(c + 1) * TPC, :])\
                      .then_inc(x_out[c], 16)
            for c in range(C):
                sp.wait_ge(x_out[c], B * 16)

        @block.gpsimd
        def _(gp):
            gp.memset(v_ring[:, :, :, HD:2 * HD], 1.0).then_inc(pool_setup, 1)
            gp.wait_ge(pool_setup, 1)
            gp.memset(k6[ROWS:AUG, :], 1.0).then_inc(pool_setup, 1)
            gp.wait_ge(pool_setup, 2)
            gp.wait_ge(setup_done, 1)

            def ffn(b, s):
                for c in range(C):
                    for a in range(KIN):
                        gp.wait_ge(k_read, s * KIN * C + KIN * c + a + 1)
                        pool.did(gp.tensor_tensor(kf[:, a, :], kf[:, a, :], kst[:, a, 0, :], ALU.subtract))
                        pool.wait(gp, b)
                        waited(gp)
                        pool.did(gp.tensor_copy(kst[:, a, 1, :], kf[:, a, :]))
                        pool.wait(gp, b)
                        gp.tensor_tensor(kst[:, a, 2, :], kf[:, a, :], kst[:, a, 1, :], ALU.subtract)\
                          .then_inc(k_parts, 1)
                gp.wait_ge(xn_ready, (s + 1) * C)
                gp.tensor_tensor(x_res[:, :, :], x_res[:, :, :],
                                 bp[:, :].unsqueeze(1).broadcast_to([P, KT, D]), ALU.add).then_inc(bp_added, 1)
                gp.wait_ge(v_read, (s + 1) * 2 * C)
                waited(gp)

                def v_slots(ch, g0):
                    group = gp.snap((ch // C) * (HPG * HD)) if not isinstance(ch, int) else (ch // C) * HPG * HD
                    for u in range(U):
                        gp.wait_ge(pv_done, g0 + u + 1)
                        waited(gp)
                        gp.tensor_copy(v_ring[:, u % VSLOTS, :, 0:HD],
                                       v_all[:, u, bass.ds(group, HPG * HD)]
                                       .rearrange("p (h d) -> p h d", h=HPG)).then_inc(v_slot, 1)

                with gp.Fori(0, NC) as i:
                    v_slots(i, (s * NC + i) * U)

            with gp.Fori(0, B) as b:
                pool.n = 0
                ffn(b, b * 2)
                for c in range(C):
                    for kt in range(KIN):
                        gp.wait_ge(r_exp, b * KIN * C + KIN * c + kt + 1)
                        waited(gp)
                        r = rt[:, kt, c * CH:(c + 1) * CH]
                        gp.tensor_scalar(r, r, 1.0, None, ALU.add).then_inc(r_den, 1)
                ffn(b, b * 2 + 1)
            counts["pool"] = pool.n

        @block.scalar
        def _(act):
            act.wait_ge(setup_step, 2)
            act.activation(temp[:, 2, :], temp[:, 2, :], ACT.Exp, scale=-1.0).then_inc(setup_step, 1)
            act.activation(decay[:, :, :], decay[:, :, :], ACT.Exp).then_inc(setup_step, 1)
            act.wait_ge(setup_step, 5)
            act.activation(temp[:, 2, :], temp[:, 2, :], ACT.Ln).then_inc(setup_step, 1)
            act.activation(decay[:, 0, :], decay[:, 0, :], ACT.Exp, scale=-1.0).then_inc(setup_step, 1)
            act.wait_ge(setup_done, 1)
            act.sem_inc(exp_done, 2)
            act.sem_inc(pv_done, VSLOTS)

            def guess(b, dst, src):
                act_steps.did(act.activation(dst, src, ACT.Ln))
                act_steps.wait(act, b)
                return act.activation(dst, dst, ACT.Exp, scale=-0.5)

            def transposed(b_c, ps_sem, sb_sem, dst, c):
                for kt in range(KIN):
                    act.wait_ge(ps_sem, b_c * KIN + kt + 1)
                    act.copy(dst[:, kt, c * CH:(c + 1) * CH], ps[:, kt, :]).then_inc(sb_sem, 1)

            def ffn(b, s):
                def parts(c, bank, kind_ps, n0, f, stage, stored, bias, done):
                    for a in range(KIN):
                        act.wait_ge(kind_ps, n0 + a + 1)
                        if c >= 1:
                            act.wait_ge(stored[a], (s * C + c) * 16)
                        act.activation(f[:, a, :], ps[:, bank + a, :], ACT.Identity,
                                       bias=bias[:, a:a + 1] if bias is not None else 0.0)
                        act.activation(stage[:, a, 0, :], ps[:, bank + a, :], ACT.Identity,
                                       bias=bias[:, a:a + 1] if bias is not None else 0.0).then_inc(done, 1)

                act.wait_ge(var_ready, s + 1)
                guess(b, rstd[:, :], mv[:, :, 1]).then_inc(rstd_ready, 1)
                transposed(s * C, xt_ps, xt_sb, xn_t, 0)
                for c in range(C):
                    n0 = s * KIN * C + KIN * c
                    for a in range(2):
                        act.wait_ge(q_added, s * 2 * C + 2 * c + a + 1)
                        act.activation(qsq[:, a, :], qn[:, a, :], ACT.Square).then_inc(q_sq, 1)
                    act.wait_ge(q_ss, s * C + c + 1)
                    guess(b, rnorm[:, 1, :], rnorm[:, 0, :]).then_inc(q_rn, 1)
                    parts(c, 4, k_ps, n0, kf, kst, k_stored, bk, k_read)
                    if c + 1 < C:
                        transposed(s * C + c + 1, xt_ps, xt_sb, xn_t, c + 1)
                    parts(c, 0, qt_ps, n0, qf, qst, q_stored, None, qt_read)

                def exp_unit(n, u):
                    for half in range(2):
                        act.wait_ge(qk_ready, 2 * (n * U + u) + half + 1)
                        if half == 0:
                            act.wait_ge(pv_done, n * U + u - 1 + VSLOTS)
                        act.activation(prob[:, u % 2, 2 * half:2 * half + 2, :],
                                       ps[:, E_BANK + 2 * half:E_BANK + 2 * half + 2, :], ACT.Exp)\
                           .then_inc(exp_done, 1)

                def copy_out(i):
                    act.wait_ge(pv_done, (s * NC + i) * U + U + VSLOTS)
                    act.copy(o_t[:, bass.ds(i * CH, CH)], ps[:, O_BANK, :]).then_inc(o_copied, 1)

                exp_unit(s * NC, 0)
                with act.Fori(0, NC - 1) as i:
                    for u in range(1, U):
                        exp_unit(s * NC + i, u)
                    exp_unit(s * NC + i + 1, 0)
                    copy_out(i)
                for u in range(1, U):
                    exp_unit(s * NC + NC - 1, u)
                copy_out(NC - 1)

                for t in range(KT):
                    if t % 2 == 0:
                        p = t // 2
                        act.wait_ge(ht_ps, s * (KT // 2) + p + 1)
                        act.copy(h_t[:, :, t * P:(t + 2) * P],
                                 ps[:, 2 + p % 2, :].rearrange("p (k t) -> p k t", k=KIN)).then_inc(ht_sb, 1)
                        if p == 0:
                            continue
                    for tt in ((t - 2, t - 1) if t % 2 == 0 else ()):
                        read_y(s, tt)
                for tt in (KT - 2, KT - 1):
                    read_y(s, tt)
                act.wait_ge(gate_in, s + 1)
                act.activation(lg[:, :, :], lg[:, :, :], ACT.Exp).then_inc(gate_exp, 1)

            def read_y(s, t):
                act.wait_ge(y_ps, s * KT + t + 1)
                act.copy(y[:, t, :], ps[:, 4 + t % 4, 0:D])
                act.copy(lg[:, t, :], ps[:, 4 + t % 4, D:NOUT]).then_inc(y_read, 1)

            with act.Fori(0, B) as b:
                act_steps.n = 0
                ffn(b, b * 2)
                act.wait_ge(a_var, b + 1)
                guess(b, rstd[:, :], mv[:, :, 1]).then_inc(a_rstd, 1)
                for t in range(KT):
                    act.wait_ge(x1_ready, b * KT + t + 1)
                    act.activation(n1[:, t, :], x1[:, t, :], ACT.Square, accum_out=msq[:, 0, t:t + 1])\
                       .then_inc(sq_done, 1)
                act.wait_ge(ms_ready, 2 * b + 1)
                guess(b, msq[:, 1, :], msq[:, 0, :]).then_inc(rms_ready, 1)
                transposed(b * C, nt_ps, nt_sb, n1_t, 0)
                for c in range(C):
                    for kt in range(KIN):
                        n = b * KIN * C + KIN * c + kt
                        act.wait_ge(kvr_ps, 2 * n + 1)
                        if c >= 1:
                            act.wait_ge(kv_read, n - KIN + 1)
                        elif True:
                            act.wait_ge(kv_read, b * KIN * C)
                        act.copy(ksb[:, kt, :], ps[:, 2 + kt, :]).then_inc(k_copied, 1)
                        act.wait_ge(kvr_ps, 2 * n + 2)
                        act.activation(rt[:, kt, c * CH:(c + 1) * CH], ps[:, 6 + kt, :], ACT.Exp, scale=-1.0)\
                           .then_inc(r_exp, 1)
                    if c + 1 < C:
                        transposed(b * C + c + 1, nt_ps, nt_sb, n1_t, c + 1)
                for t in range(KT):
                    act.wait_ge(x2_ready, b * C * 2 + t // 2 + 1)
                    act.activation(n1[:, t, :], x1[:, t, :], ACT.Square, accum_out=msq[:, 0, t:t + 1])\
                       .then_inc(sq2_done, 1)
                act.wait_ge(ms_ready, 2 * b + 2)
                guess(b, msq[:, 1, :], msq[:, 0, :]).then_inc(rms2_ready, 1)
                transposed(b * C, mt_ps, mt_sb, n1_t, 0)
                def square(n):
                    c, j = divmod(n, HT)
                    act.wait_ge(fc_read, b * HT * C + n + 1)
                    if c >= 2:
                        act.wait_ge(out_ps, b * 2 * C + 2 * (c - 1))
                    act.activation(hid[:, c % 2, j, :], z_relu[:, j % 2, :], ACT.Square, scale=0.5)\
                       .then_inc(hid_ready, 1)

                for c in range(C):
                    for j in range(HT):
                        n = HT * c + j
                        act.wait_ge(fc_ps, b * HT * C + n + 1)
                        if n >= 2:
                            act.wait_ge(hid_ready, b * HT * C + n - 1)
                        act.activation(z_relu[:, j % 2, :], ps[:, 2 + j % 4, :], ACT.Relu).then_inc(fc_relu, 1)
                        if n >= 1:
                            square(n - 1)
                    if c + 1 < C:
                        transposed(b * C + c + 1, mt_ps, mt_sb, n1_t, c + 1)
                square(HT * C - 1)
                ffn(b, b * 2 + 1)
            counts["act"] = act_steps.n

        @block.vector
        def _(ve):
            ve.wait_ge(consts_in, 16 * NCONST)
            ve.wait_ge(pool_setup, 2)
            ve.tensor_copy(ident_bf[:, :], ident[:, :])
            ve.tensor_scalar(temp[:, 3, :], temp[:, 1, :], -1.0, None, ALU.mult).then_inc(setup_step, 1)
            ve.wait_ge(setup_step, 1)
            ve.tensor_tensor(temp[:, 2, :], temp[:, 1, :], temp[:, 3, :], ALU.max).then_inc(setup_step, 1)
            ve.tensor_tensor(ao[:, :, :], ao[:, :, :], mixs[:, :].unsqueeze(1).broadcast_to([P, KIN, D]), ALU.mult)
            ve.tensor_tensor(wmlp[:, :, :], wmlp[:, :, :], mlps[:, :].unsqueeze(1).broadcast_to([P, HT, D]), ALU.mult)
            ve.tensor_scalar(bp[:, :], bp[:, :], 0.5, None, ALU.mult)
            ve.wait_ge(setup_step, 4)
            ve.tensor_scalar(temp[:, 2, :], temp[:, 2, :], 1.0, None, ALU.add).then_inc(setup_step, 1)
            ve.wait_ge(setup_step, 7)
            ve.scalar_tensor_tensor(temp[:, 0, :], temp[:, 1, :], 0.0, temp[:, 2, :], ALU.max, ALU.add)\
              .then_inc(setup_step, 1)
            ve.wait_ge(setup_step, 8)
            ve.tensor_scalar(temp[:, 0, :], temp[:, 0, :], HD ** -0.5, None, ALU.mult).then_inc(setup_step, 1)
            ve.wait_ge(setup_step, 9)
            ve.tensor_tensor(embs[:, :].rearrange("p (h d) -> p h d", h=H), embs[:, :].rearrange("p (h d) -> p h d", h=H),
                             temp[:, 0, :].unsqueeze(2).broadcast_to([P, H, HD]), ALU.mult).then_inc(setup_step, 1)
            ve.wait_ge(setup_step, 10)
            ve.memset(st[:, :, :, 0:1], 0.0).then_inc(setup_done, 1)

            def link(ins, b):
                dve.did(ins)
                dve.wait(ve, b)

            def statistics(b, src, signal, arrived=None):
                ready = []
                for t in range(KT):
                    if arrived is not None and t % TPC == 0:
                        ve.wait_ge(x_in[t // TPC], (b + 1) * 16)
                    ready.append(dve.did(ve.bn_stats(bn[:, t, :], src[:, t, :])))
                for t in range(KT):
                    dve.wait(ve, b, ready[t])
                    waited(ve)
                    ins = ve.bn_aggr(mv[:, t, :], bn[:, t, :])
                link(ins, b)
                ve.tensor_scalar(mv[:, :, 1], mv[:, :, 1], LN_EPS, None, ALU.add).then_inc(signal, 1)

            def refine(b, y, x, tmp):
                link(ve.tensor_tensor(tmp, x, y, ALU.mult), b)
                link(ve.tensor_tensor(tmp, tmp, y, ALU.mult), b)
                link(ve.tensor_scalar(tmp, tmp, -0.5, 1.5, ALU.mult, ALU.add), b)
                link(ve.tensor_tensor(y, y, tmp, ALU.mult), b)

            def heads(ap, t):
                return ap.rearrange("p (t h d) -> p t h d", t=t, h=H)

            def ffn(b, s, layer):
                statistics(b, x_res, var_ready, arrived=True if layer == 0 else None)
                ve.wait_ge(rstd_ready, s + 1)
                refine(b, rstd[:, :], mv[:, :, 1], newton[:, 0:KT])
                for t in range(KT):
                    ins = ve.tensor_scalar(xn[:, t, :], x_res[:, t, :], mv[:, t, 0:1], rstd[:, t:t + 1],
                                           ALU.subtract, ALU.mult)
                    if t % TPC == TPC - 1:
                        ins.then_inc(xn_ready, 1)
                for c in range(C):
                    for a in range(2):
                        n = s * 2 * C + 2 * c + a
                        ve.wait_ge(q_ps, n + 1)
                        if c >= 1:
                            ve.wait_ge(qt_ps, s * KIN * C + KIN * c)
                        ve.tensor_tensor(qn[:, a, :].rearrange("p (t d) -> p t d", t=2),
                                         ps[:, 2 + a, :].rearrange("p (t d) -> p t d", t=2),
                                         bq[:, :].unsqueeze(1).broadcast_to([P, 2, D]), ALU.add).then_inc(q_added, 1)
                    for a in range(2):
                        ve.wait_ge(q_sq, s * 2 * C + 2 * c + a + 1)
                        last = ve.tensor_reduce(rnorm[:, 0, a * 2 * H:(a + 1) * 2 * H].rearrange("p (t h) -> p t h", t=2),
                                                heads(qsq[:, a, :], 2), AX.X, ALU.add)
                    last.then_inc(q_ss, 1)
                    for a in range(2):
                        n = s * 2 * C + 2 * c + a
                        ve.wait_ge(v_ps, n + 1)
                        ve.tensor_tensor(v_all[:, c * TPC + 2 * a:c * TPC + 2 * a + 2, :],
                                         ps[:, 6 + a, :].rearrange("p (t d) -> p t d", t=2),
                                         bv[:, :].unsqueeze(1).broadcast_to([P, 2, D]), ALU.add).then_inc(v_read, 1)
                    ve.wait_ge(q_rn, s * C + c + 1)
                    refine(b, rnorm[:, 1, :], rnorm[:, 0, :], newton[:, :])
                    by_head = rnorm[:, 1, :].rearrange("p (t h) -> p t h", h=H)
                    link(ve.tensor_tensor(by_head, by_head, temp[:, 0:1, :].broadcast_to([P, TPC, H]), ALU.mult), b)
                    for a in range(2):
                        scale = rnorm[:, 1, a * 2 * H:(a + 1) * 2 * H].rearrange("p (t h) -> p t h", t=2).unsqueeze(3)\
                            .broadcast_to([P, 2, H, HD])
                        k1 = dve.did(ve.tensor_tensor(heads(qn[:, a, :], 2), heads(qn[:, a, :], 2), scale, ALU.mult))
                        dve.wait(ve, b, k1)
                        v2 = qn[:, a, :].rearrange("p (t d) -> p t d", t=2)
                        ve.tensor_tensor(v2, v2, embs[:, :].unsqueeze(1).broadcast_to([P, 2, D]), ALU.add)\
                          .then_inc(q_done, 1)
                    for a in range(KIN):
                        ve.wait_ge(qt_read, s * KIN * C + KIN * c + a + 1)
                        k1 = dve.did(ve.tensor_tensor(qf[:, a, :], qf[:, a, :], qst[:, a, 0, :], ALU.subtract))
                        dve.wait(ve, b, k1)
                        k2 = dve.did(ve.tensor_copy(qst[:, a, 1, :], qf[:, a, :]))
                        dve.wait(ve, b, k2)
                        ve.tensor_tensor(qst[:, a, 2, :], qf[:, a, :], qst[:, a, 1, :], ALU.subtract)\
                          .then_inc(q_parts, 1)

                def elements(base, count, mt, n, tile, turn=0):
                    split = []
                    for e in range(count):
                        bank = M_BANK + (e + turn) % M_BANKS
                        ve.wait_ge(max_ready, base + e + 1)
                        if e == mt:
                            ve.wait_ge(mrow_in, 16 * n)
                            ve.tensor_copy(mrow[:, :], ps[0:3 * HPG, bank, 0:CH // 2].bitcast(BF16))\
                              .then_inc(mrow_ready, 1)
                            ve.wait_ge(mrow_ready, n + 1)
                            ve.sem_inc(max_free, 1)
                            continue
                        ve.tensor_reduce(pmax[:, tile:tile + 1], ps[:, bank, :], AX.X, ALU.max).then_inc(max_free, 1)
                        tile += 1
                        if tile == HPG * TPC * C:
                            ve.wait_ge(max_free, base + e + 1)
                            ve.tensor_reduce(negm[:, 0, :], pmax[:, :].rearrange("p (x c) -> p x c", c=C), AX.X,
                                             ALU.max, negate=True).then_inc(m_step, 1)
                            ve.wait_ge(m_step, 5 * n + 1)
                            split = [0, 1, 2, 3]
                            tile = 0
                        elif split:
                            split_max(n, split.pop(0))

                def split_max(n, step):
                    parts = mparts[:, :].rearrange("p (q r h) -> p r h q", r=3, h=HPG)
                    neg = [negm[:, j, :].rearrange("p (h q) -> p h q", h=HPG) for j in range(2)]
                    ve.wait_ge(m_step, 5 * n + 1 + step)
                    if step == 0:
                        ve.tensor_copy(parts[:, 0, :, :], neg[0]).then_inc(m_step, 1)
                    if step == 1:
                        ve.tensor_tensor(neg[1], neg[0], parts[:, 0, :, :], ALU.subtract).then_inc(m_step, 1)
                    if step == 2:
                        ve.tensor_copy(parts[:, 1, :, :], neg[1]).then_inc(m_step, 1)
                    if step == 3:
                        ve.tensor_tensor(parts[:, 2, :, :], neg[1], parts[:, 1, :, :], ALU.subtract).then_inc(m_step, 1)

                elements(s * RING_STAGE, RING_PRO, MT_PRO, s * NC, 0, RING_TURN)
                with ve.Fori(0, NC - 1) as i:
                    elements(s * RING_STAGE + RING_PRO + i * RING_BODY, RING_BODY, MT_BODY, s * NC + i + 1, 4 * LEAD)

                for t in range(KT):
                    ve.wait_ge(on_ps, s * KT + t + 1)
                    o = ps[:, t % 2, :].rearrange("p (h e) -> p h e", h=H)
                    k1 = dve.did(ve.reciprocal(rden[:, t, :].unsqueeze(2), o[:, :, HD:HD + 1]))
                    dve.wait(ve, b, k1)
                    ve.tensor_tensor(hn[:, t, :].rearrange("p (h d) -> p h d", h=H), o[:, :, 0:HD],
                                     rden[:, t, :].unsqueeze(2).broadcast_to([P, H, HD]), ALU.mult)\
                      .then_inc(hn_ready, 1)
                ve.wait_ge(y_read, (s + 1) * KT)

                routed, shared = lg[:, :, 0:NGATE], lg[:, :, NGATE:NG]
                col = [gsm[:, j, :].unsqueeze(2) for j in range(8)]
                link(ve.tensor_tensor(lg[:, :, :], lg[:, :, :], brs[:, :].unsqueeze(1).broadcast_to([P, KT, NG]), ALU.add), b)
                ve.tensor_reduce(col[0], routed, AX.X, ALU.max)
                link(ve.tensor_reduce(col[1], shared, AX.X, ALU.max), b)
                link(ve.tensor_tensor(routed, routed, col[0].broadcast_to([P, KT, NGATE]), ALU.subtract), b)
                ve.tensor_tensor(shared, shared, col[1].broadcast_to([P, KT, NSH]), ALU.subtract).then_inc(gate_in, 1)
                ve.wait_ge(gate_exp, s + 1)
                link(ve.tensor_reduce(col[2], routed, AX.X, ALU.add), b)
                dve.did(ve.tensor_reduce(col[3], shared, AX.X, ALU.add))
                for t in range(KT):
                    last = ve.max(top[:, t, :], lg[:, t, 0:NGATE])
                link(last, b)
                link(ve.tensor_reduce(col[4], top[:, :, 0:TOPK], AX.X, ALU.add), b)
                link(ve.reciprocal(gsm[:, 2:4, :], gsm[:, 2:4, :]), b)
                link(ve.tensor_tensor(col[4], col[4], col[2], ALU.mult), b)
                link(ve.tensor_tensor(sw[:, :, :], shared, col[3].broadcast_to([P, KT, NSH]), ALU.mult), b)
                link(ve.tensor_tensor(col[5], sw[:, :, 0:1], sw[:, :, 1:2], ALU.add), b)
                link(ve.tensor_tensor(col[5], col[5], sw[:, :, 0:1], ALU.mult), b)
                link(ve.scalar_tensor_tensor(col[6], col[4], float(TOPK), sw[:, :, 1:2], ALU.mult, ALU.mult), b)
                link(ve.tensor_tensor(col[7], col[5], col[6], ALU.add), b)
                ve.wait_ge(bp_added, s + 1)
                for t in range(KT):
                    last = ve.scalar_tensor_tensor(x_res[:, t, :], y[:, t, :], gsm[:, 7, t:t + 1], x_res[:, t, :],
                                                   ALU.mult, ALU.add)
                    if layer == 1 and t % TPC == TPC - 1:
                        last.then_inc(x_final, 1)
                if layer == 0:
                    link(last, b)

            def inv_rms(b, squares, ready):
                ve.wait_ge(squares, (b + 1) * KT)
                ve.tensor_scalar(msq[:, 0, :], msq[:, 0, :], 1.0 / D, RMS_EPS, ALU.mult, ALU.add).then_inc(ms_ready, 1)
                ve.wait_ge(ready, b + 1)
                refine(b, msq[:, 1, :], msq[:, 0, :], newton[:, 0:KT])

            def recurrence(b):
                statistics(b, x_res, a_var)
                ve.wait_ge(a_rstd, b + 1)
                refine(b, rstd[:, :], mv[:, :, 1], newton[:, 0:KT])
                for t in range(KT):
                    ve.tensor_scalar(x1[:, t, :], x_res[:, t, :], mv[:, t, 0:1], rstd[:, t:t + 1],
                                     ALU.subtract, ALU.mult).then_inc(x1_ready, 1)
                inv_rms(b, sq_done, rms_ready)
                for t in range(KT):
                    last = ve.tensor_scalar(n1[:, t, :], x1[:, t, :], msq[:, 1, t:t + 1], None, ALU.mult)
                    if t % TPC == TPC - 1:
                        last.then_inc(n1_ready, 1)

                def add_mix(c):
                    for a in range(2):
                        ve.wait_ge(mix_ps, b * 2 * C + 2 * c + a + 1)
                        x = x1[:, c * TPC + 2 * a:c * TPC + 2 * a + 2, :]
                        ve.tensor_tensor(x, x, ps[:, a, :].rearrange("p (t d) -> p t d", t=2), ALU.add)\
                          .then_inc(x2_ready, 1)

                for c in range(C):
                    span = slice(c * CH, (c + 1) * CH)
                    kv = [rw[:, kt, span] for kt in range(KIN)]
                    for kt in range(KIN):
                        n = b * KIN * C + KIN * c + kt
                        ve.wait_ge(k_copied, n + 1)
                        dve.did(ve.tensor_tensor(kv[kt], ps[:, 4 + kt, :], ksb[:, kt, :], ALU.mult))
                        dve.wait(ve, b)
                        if c >= 1:
                            dve.did(ve.tensor_copy(st[:, c % 2, kt, 0:1], st[:, (c - 1) % 2, kt, CH:CH + 1]))
                        else:
                            dve.did(ve.memset(st[:, 0, kt, 0:1], 0.0))
                        dve.wait(ve, b)
                        dve.did(ve.tensor_tensor_scan(st[:, c % 2, kt, 1:CH + 1],
                                                      decay[:, 0, kt:kt + 1].broadcast_to([P, CH]), kv[kt],
                                                      st[:, c % 2, kt, 0:1], ALU.mult, ALU.add))
                        dve.wait(ve, b)
                        ve.scalar_tensor_tensor(kv[kt], kv[kt], decay[:, 1, kt:kt + 1], st[:, c % 2, kt, 0:CH],
                                                ALU.mult, ALU.add).then_inc(kv_read, 1)
                    for kt in range(KIN):
                        n = b * KIN * C + KIN * c + kt
                        ve.wait_ge(r_den, n + 1)
                        dve.did(ve.reciprocal(rt[:, kt, span], rt[:, kt, span]))
                        dve.wait(ve, b)
                        ve.wait_ge(kv_read, n + 1)
                        ve.tensor_tensor(kv[kt], kv[kt], rt[:, kt, span], ALU.mult).then_inc(rw_ready, 1)
                    if c >= 1:
                        add_mix(c - 1)
                add_mix(C - 1)
                inv_rms(b, sq2_done, rms2_ready)
                for t in range(KT):
                    last = ve.tensor_scalar(n1[:, t, :], x1[:, t, :], msq[:, 1, t:t + 1], None, ALU.mult)
                    if t % TPC == TPC - 1:
                        last.then_inc(n2_ready, 1)
                for c in range(C):
                    xs = x_res[:, c * TPC:(c + 1) * TPC, :]
                    dve.did(ve.tensor_tensor(xs, xs, x1[:, c * TPC:(c + 1) * TPC, :], ALU.add))
                def add_out(c):
                    for a in range(2):
                        ve.wait_ge(out_ps, b * 2 * C + 2 * c + a + 1)
                        x = x_res[:, c * TPC + 2 * a:c * TPC + 2 * a + 2, :]
                        dve.wait(ve, b)
                        ve.tensor_tensor(x, x, ps[:, 6 + a, :].rearrange("p (t d) -> p t d", t=2), ALU.add)\
                          .then_inc(out_read, 1)

                for c in range(C):
                    for j in range(HT):
                        ve.wait_ge(fc_relu, b * HT * C + HT * c + j + 1)
                        ve.tensor_tensor(z_relu[:, j % 2, :], z_relu[:, j % 2, :], ps[:, 2 + j % 4, :], ALU.add)\
                          .then_inc(fc_read, 1)
                    if c >= 1:
                        add_out(c - 1)
                add_out(C - 1)
                ve.wait_ge(out_read, (b + 1) * 2 * C)

            with ve.Fori(0, B) as b:
                dve.n = 0
                ffn(b, b * 2, 0)
                recurrence(b)
                ffn(b, b * 2 + 1, 1)
            counts["dve"] = dve.n

        @block.tensor
        def _(pe):
            pe.wait_ge(setup_done, 1)

            def transposes(c, src, ready, ready_at, signal, banks=(0, 1)):
                pe.wait_ge(ready, ready_at)
                for kt in range(KIN):
                    for j in range(TPC):
                        last = pe.transpose(ps[:, banks[kt], j * P:(j + 1) * P],
                                            src[:, c * TPC + j, kt * P:(kt + 1) * P], ident[:, :])
                    last.then_inc(signal, 1)

            def natural(c, a, w, acts, bank, signal):
                for j in range(2):
                    t = c * TPC + 2 * a + j
                    for kt in range(KIN):
                        last = pe.matmul(ps[:, bank, j * D:(j + 1) * D], acts[:, kt, t * P:(t + 1) * P], w[:, kt, :],
                                         start=kt == 0, stop=kt == KIN - 1)
                last.then_inc(signal, 1)

            def columns(c, m, w, acts, bank):
                for kt in range(KIN):
                    last = pe.matmul(ps[:, bank, :], w[:, kt, m * P:(m + 1) * P], acts[:, kt, c * CH:(c + 1) * CH],
                                     start=kt == 0, stop=kt == KIN - 1)
                return last

            def ffn(s):
                transposes(0, xn, xn_ready, s * C + 1, xt_ps)
                for c in range(C):
                    n = s * 2 * C + 2 * c
                    pe.wait_ge(xt_sb, n + 2)
                    for a in range(2):
                        if c >= 1:
                            pe.wait_ge(q_added, n - 2 + a + 1)
                        natural(c, a, wq, xn_t, 2 + a, q_ps)
                    for a in range(KIN):
                        if c >= 1:
                            pe.wait_ge(k_read, n - 2 + a + 1)
                        columns(c, a, wk, xn_t, 4 + a).then_inc(k_ps, 1)
                    for a in range(2):
                        if c >= 1:
                            pe.wait_ge(v_read, n - 2 + a + 1)
                        natural(c, a, wv, xn_t, 6 + a, v_ps)
                    if c + 1 < C:
                        if c >= 1:
                            pe.wait_ge(qt_read, n)
                        transposes(c + 1, xn, xn_ready, s * C + c + 2, xt_ps)
                        pe.wait_ge(xt_sb, n + 4)
                    pe.wait_ge(q_done, n + 2)
                    for kt in range(KIN):
                        for j in range(TPC):
                            a, t = divmod(j, 2)
                            last = pe.transpose(ps[:, kt, j * P:(j + 1) * P],
                                                qn[:, a, t * D + kt * P:t * D + (kt + 1) * P], ident[:, :])
                        last.then_inc(qt_ps, 1)

                n = (s + 1) * 2 * C
                for sm in (qt_read, k_read, v_read):
                    pe.wait_ge(sm, n)

                def offsets(ch):
                    at_k = ((ch // C) % 2) * (HPG * S)
                    at_q = at_k + (ch % C) * CH
                    return (at_k, at_q) if isinstance(ch, int) else (pe.snap(at_k), pe.snap(at_q))

                def scores(at, u, half, n):
                    pe.wait_ge(exp_done, 2 * (n * U + u) + half + 1)
                    for h in (2 * half, 2 * half + 1):
                        last = pe.matmul(ps[:, E_BANK + h, :], k6[0:AUG, bass.ds(at[0] + h * S + u * P, P)],
                                         q6[0:AUG, bass.ds(at[1] + h * S, CH)], start=True, stop=True)
                    last.then_inc(qk_ready, 1)

                def element(base, e, mt, m_at, at, tile, turn=0):
                    back = e - M_BANKS + 1 if e >= M_BANKS else -((RING_BODY - 1 - e) % M_BANKS)
                    if not (mt == MT_PRO and e < M_BANKS):
                        pe.wait_ge(max_free, base + back)
                    bank = M_BANK + (e + turn) % M_BANKS
                    if e == mt:
                        pe.wait_ge(m_step, 5 * m_at + 5)
                        waited(pe)
                        for x in range(TPC):
                            last = pe.transpose(ps[0:3 * HPG, bank, x * P // 2:(x + 1) * P // 2].bitcast(BF16),
                                                mparts[:, x * 3 * HPG:(x + 1) * 3 * HPG], ident_bf[:, :])
                        last.then_inc(max_ready, 1)
                        return
                    x, kc = divmod(tile, C)
                    h, qt = divmod(x, TPC)
                    pe.matmul(ps[:, bank, :], q6[0:ROWS, bass.ds(at[1] + h * S + qt * P, P)],
                              k6[0:ROWS, bass.ds(at[0] + h * S + kc * CH, CH)], start=True, stop=True)\
                      .then_inc(max_ready, 1)

                def products(u, n):
                    pe.wait_ge(exp_done, 2 * (n * U + u) + 4)
                    pe.wait_ge(v_slot, n * U + u + 1)
                    if u == 0:
                        pe.wait_ge(o_copied, n)
                    for h in range(HPG):
                        last = pe.matmul(ps[32 * h:32 * h + 2 * HD, O_BANK, :], v_ring[:, u % VSLOTS, h, :],
                                         prob[:, u % 2, h, :], start=u == 0, stop=u == U - 1)
                    last.then_inc(pv_done, 1)

                NT = HPG * TPC * C
                pe.wait_ge(ops_loaded, 32 * NPROD * (s * HG + 1))
                at0, at1 = offsets(0), offsets(1)
                tile = 0
                for e in range(RING_PRO):
                    first = e < NT
                    if e == NT and 1 // C > 0:
                        pe.wait_ge(ops_loaded, 32 * NPROD * (s * HG + 2))
                    element(s * RING_STAGE, e, MT_PRO, s * NC, at0 if first else at1, tile % NT, RING_TURN)
                    tile += e != MT_PRO
                pe.wait_ge(mrow_in, 16 * (s * NC + 1))
                for half in range(2):
                    scores(at0, 0, half, s * NC)

                with pe.Fori(0, NC - 1) as i:
                    n = s * NC + i
                    here, ahead, ahead2 = offsets(i), offsets(i + 1), offsets((i + 2) % NC)
                    base = s * RING_STAGE + RING_PRO + i * RING_BODY
                    tile, e = 4 * LEAD, 0
                    for u in range(U):
                        if u == U - 1:
                            pe.wait_ge(mrow_in, 16 * (n + 2))
                        for half in range(2):
                            if u < U - 1:
                                scores(here, u + 1, half, n)
                            else:
                                scores(ahead, 0, half, n + 1)
                            for _ in range(2 + (u == U - 1 and half == 1)):
                                if tile == NT:
                                    pe.wait_ge(ops_loaded, 32 * NPROD * (s * HG + ((i + 2) % NC) // C + 1))
                                element(base, e, MT_BODY, n + 1, ahead if tile < NT else ahead2, tile % NT)
                                tile += e != MT_BODY
                                e += 1
                        products(u, n)
                n = s * NC + NC - 1
                at = offsets(NC - 1)
                for u in range(U):
                    if u < U - 1:
                        for half in range(2):
                            scores(at, u + 1, half, n)
                    products(u, n)

                pe.wait_ge(o_copied, (s + 1) * NC)
                pe.wait_ge(max_free, (s + 1) * RING_STAGE)

                def turn(t):
                    if t >= 2:
                        pe.wait_ge(hn_ready, s * KT + t - 1)
                    for hg in range(HG):
                        last = pe.transpose(ps[:, t % 2, hg * P:(hg + 1) * P], o_t[:, hg * S + t * P:hg * S + (t + 1) * P],
                                            ident[:, :])
                    last.then_inc(on_ps, 1)

                def back(p):
                    pe.wait_ge(hn_ready, s * KT + 2 * p + 2)
                    if p >= 2:
                        pe.wait_ge(ht_sb, s * (KT // 2) + p - 1)
                    for j in range(2):
                        for kt in range(KIN):
                            last = pe.transpose(ps[:, 2 + p % 2, kt * 2 * P + j * P:kt * 2 * P + (j + 1) * P],
                                                hn[:, 2 * p + j, kt * P:(kt + 1) * P], ident[:, :])
                    last.then_inc(ht_ps, 1)

                def project(t):
                    pe.wait_ge(ht_sb, s * (KT // 2) + t // 2 + 1)
                    if t >= 4:
                        pe.wait_ge(y_read, s * KT + t - 3)
                    for kt in range(KIN):
                        last = pe.matmul(ps[:, 4 + t % 4, 0:NOUT], h_t[:, kt, t * P:(t + 1) * P], wprs[:, kt, :],
                                         start=kt == 0, stop=kt == KIN - 1)
                    last.then_inc(y_ps, 1)

                turn(0)
                turn(1)
                for p in range(KT // 2):
                    if 2 * p + 2 < KT:
                        turn(2 * p + 2)
                        turn(2 * p + 3)
                    back(p)
                    if p >= 1:
                        project(2 * p - 2)
                        project(2 * p - 1)
                project(KT - 2)
                project(KT - 1)
                pe.wait_ge(y_read, (s + 1) * KT)

            def recurrence(b):
                transposes(0, n1, n1_ready, b * C + 1, nt_ps)

                def mix(c):
                    pe.wait_ge(rw_ready, b * KIN * C + KIN * (c + 1))
                    if c + 2 < C:
                        pe.wait_ge(nt_sb, b * KIN * C + KIN * (c + 3))
                    else:
                        pe.wait_ge(nt_sb, (b + 1) * KIN * C)
                    for a in range(2):
                        if c >= 1:
                            pe.wait_ge(x2_ready, b * 2 * C + 2 * (c - 1) + a + 1)
                        natural(c, a, ao, rw, a, mix_ps)

                for c in range(C):
                    n = b * KIN * C + KIN * c
                    pe.wait_ge(nt_sb, n + KIN)
                    for kt in range(KIN):
                        if c >= 1:
                            pe.wait_ge(kv_read, n - KIN + kt + 1)
                            pe.wait_ge(r_exp, n - KIN + kt + 1)
                        columns(c, kt, ak, n1_t, 2 + kt)
                        columns(c, kt, av, n1_t, 4 + kt).then_inc(kvr_ps, 1)
                        columns(c, kt, ar, n1_t, 6 + kt).then_inc(kvr_ps, 1)
                    if c + 1 < C:
                        if c >= 2:
                            pe.wait_ge(x2_ready, b * 2 * C + 2 * (c - 1))
                        transposes(c + 1, n1, n1_ready, b * C + c + 2, nt_ps)
                    if c >= 1:
                        mix(c - 1)
                mix(C - 1)
                pe.wait_ge(x2_ready, (b + 1) * 2 * C)
                transposes(0, n1, n2_ready, b * C + 1, mt_ps)

                def down(c):
                    pe.wait_ge(hid_ready, b * HT * C + HT * (c + 1))
                    for a in range(2):
                        if c >= 1:
                            pe.wait_ge(out_read, b * 2 * C + 2 * (c - 1) + a + 1)
                        for j in range(2):
                            t = 2 * a + j
                            for m in range(HT):
                                last = pe.matmul(ps[:, 6 + a, j * D:(j + 1) * D], hid[:, c % 2, m, t * P:(t + 1) * P],
                                                 wmlp[:, m, :], start=m == 0, stop=m == HT - 1)
                        last.then_inc(out_ps, 1)

                for c in range(C):
                    pe.wait_ge(mt_sb, b * KIN * C + KIN * (c + 1))
                    for m in range(HT):
                        n = HT * c + m
                        if n >= 4:
                            pe.wait_ge(fc_read, b * HT * C + n - 3)
                        columns(c, m, wfc, n1_t, 2 + m % 4).then_inc(fc_ps, 1)
                    if c + 1 < C:
                        transposes(c + 1, n1, n2_ready, b * C + c + 2, mt_ps)
                    if c >= 1:
                        down(c - 1)
                down(C - 1)
                pe.wait_ge(out_read, (b + 1) * 2 * C)

            with pe.Fori(0, B) as b:
                ffn(b * 2)
                recurrence(b)
                ffn(b * 2 + 1)
    return counts


def kernel(**inputs):
    import numpy as np
    import concourse.bacc as bacc
    from concourse import mybir as _mybir
    from concourse.bass_utils import run_bass_kernel_spmd as _run

    def arr(name):
        return np.asarray(inputs[name])

    def turned(name):
        return np.ascontiguousarray(arr(name).T)

    def columns_of(*names):
        return np.ascontiguousarray(np.stack([arr(n).reshape(2, 128).T for n in names], axis=1))

    host = {
        "x": np.ascontiguousarray(arr("L0_attn_x")),
        "ident": np.eye(128, dtype=np.float32),
        "wq_t": turned("L0_ffn_Wq"), "wk_t": turned("L0_ffn_Wk"), "wv_t": turned("L0_ffn_Wv"),
        "wp_t": turned("L0_ffn_Wp"), "wr_t": turned("L0_ffn_Wr"), "ws_t": turned("L0_ffn_Ws"),
        "ak_t": turned("L0_attn_Wk"), "av_t": turned("L0_attn_Wv"), "ar_t": turned("L0_attn_Wr"),
        "ao_t": turned("L0_attn_Wo"), "wfc_t": turned("L0_attn_Wfc"), "wmlp_t": turned("L0_attn_Wmlp"),
        "bq": arr("L0_ffn_bq"), "bv": arr("L0_ffn_bv"), "bp": arr("L0_ffn_bp"),
        "br": arr("L0_ffn_br"), "bs": arr("L0_ffn_bs"),
        "emb": np.ascontiguousarray(arr("L0_ffn_query_embedding").reshape(-1)),
        "temp": np.ascontiguousarray(arr("L0_ffn_temperature").reshape(-1)),
        "mix": arr("L0_attn_mixer_scale"), "mlp": arr("L0_attn_mlp_scale"),
        "bk_cols": np.ascontiguousarray(arr("L0_ffn_bk").reshape(2, 128).T),
        "decay_cols": columns_of("L0_attn_time_decay", "L0_attn_time_first"),
    }
    B, S, _ = host["x"].shape

    def program(totals):
        nc = bacc.Bacc("TRN2", target_bir_lowering=False, num_devices=1)
        io = {n: nc.dram_tensor(f"in_{n}", a.shape, _mybir.dt.from_np(a.dtype), kind="ExternalInput").ap()
              for n, a in host.items()}
        io["out"] = nc.dram_tensor("out_0", host["x"].shape, _mybir.dt.float32, kind="ExternalOutput").ap()
        return nc, build(nc, io, B, S, totals)

    _, totals = program({})
    nc, again = program(totals)
    assert again == totals
    r = _run(nc, [{f"in_{n}": a for n, a in host.items()}], core_ids=[0])
    return r.results[0]["out_0"]
```

```python
import math
from contextlib import ExitStack

import concourse.bass as bass
from concourse import mybir

F32 = mybir.dt.float32
BF16 = mybir.dt.bfloat16
ACT = mybir.ActivationFunctionType
ALU = mybir.AluOpType
AX = mybir.AxisListType

P = 128
D = 256
KIN = D // P
H, HD = 16, 16
HPG = 4
HG = H // HPG
CH = 512
TPC = CH // P
HID = 1024
HT = HID // P
NGATE, NSH = 15, 2
TOPK = 3
LN_RANGE = 62
LN_EPS, RMS_EPS = 1e-5, 1e-6
LEAD = 5
MT_LAG = 8
Q_PART = (0, 0, 1, 0, 2, 1)
K_PART = (0, 1, 0, 2, 0, 1)
NPROD = len(Q_PART)
ROWS = NPROD * HD
AUG = ROWS + 3
VSLOTS = 4
E_BANK, O_BANK, M_BANK = 0, 4, 5
M_BANKS = 3
LN_SET, LN_EXP_SET = 5, 6


class Steps:

    def __init__(self, sem, per_batch):
        self.sem, self.per_batch, self.n = sem, per_batch, 0
        self.before = 0

    def did(self, ins):
        ins.then_inc(self.sem, 1)
        self.n += 1
        return self.n

    def wait(self, eng, b, n=None):
        eng.wait_ge(self.sem, self.before + b * self.per_batch + (self.n if n is None else n))


def build(nc, io, B, S, totals):
    C = S // CH
    KT = S // P
    U = KT
    NC = HG * C
    assert S % CH == 0 and U > LEAD and C % 2 == 0
    RING_PRO = 4 * (U + LEAD) + 1
    RING_BODY = 4 * U + 1
    RING_STAGE = RING_PRO + (NC - 1) * RING_BODY
    RING_TURN = (RING_BODY - RING_PRO) % M_BANKS
    MT_PRO, MT_BODY = 4 * U + MT_LAG, 4 * (U - LEAD) + MT_LAG
    counts = {}

    with ExitStack() as ctx:
        def sb(name, shape, dt=F32):
            return ctx.enter_context(nc.sbuf_tensor(name, shape, dt))

        def sem(name):
            return ctx.enter_context(nc.semaphore(name))

        ident = sb("ident", [P, P])
        ident_bf = sb("ident_bf", [P, P], BF16)
        wq, wk, wv = (sb(n, [P, KIN, D]) for n in ("wq", "wk", "wv"))
        NOUT = D + NGATE + NSH
        wprs = sb("wprs", [P, KIN, NOUT])
        ak, av, ar, ao = (sb(n, [P, KIN, D]) for n in ("ak", "av", "ar", "ao"))
        wfc = sb("wfc", [P, KIN, HID])
        wmlp = sb("wmlp", [P, HT, D])
        bq, bv, bp = (sb(n, [P, D]) for n in ("bq", "bv", "bp"))
        embs = sb("embs", [P, D])
        brs = sb("brs", [P, NGATE + NSH])
        bk = sb("bk", [P, KIN])
        temp = sb("temp", [P, 4, H])
        mixs, mlps = sb("mixs", [P, D]), sb("mlps", [P, D])
        decay = sb("decay", [P, 2, KIN])
        x_res = sb("x_res", [P, KT, D])
        bn = sb("bn", [P, KT, 6])
        mv = sb("mv", [P, KT, 2])
        var_eps = sb("var_eps", [P, KT])
        ln_shift = sb("ln_shift", [P, 1])
        rstd = sb("rstd", [P, KT])
        msq = sb("msq", [P, 2, KT])
        k6 = sb("k6", [P, 2 * HPG * S], BF16)
        v_ring = sb("v_ring", [P, VSLOTS, HPG, 2 * HD])
        pmax = sb("pmax", [P, HPG * TPC * C])
        negm = sb("negm", [P, 2, HPG * TPC])
        mparts = sb("mparts", [P, 3 * HPG * TPC], BF16)
        mrow = sb("mrow", [3 * HPG, CH], BF16)
        rden = sb("rden", [P, KT, H])
        rnorm = sb("rnorm", [P, 2, TPC * H])
        newton = sb("newton", [P, TPC * H])
        NG = NGATE + NSH
        lg = sb("lg", [P, KT, NG])
        gsm = sb("gsm", [P, 8, KT])
        sw = sb("sw", [P, KT, NSH])
        top = sb("top", [P, KT, 8])
        R = HT * CH
        work = sb("work", [P, 6 * R])
        assert KT * D <= R and HPG * S <= 2 * R

        def region(first, words=KT * D):
            return work[:, first * R:first * R + words]

        q6 = region(0, HPG * S).bitcast(BF16)
        o_t = region(2, HG * S)
        prob = region(4, 2 * HPG * CH).rearrange("p (s h q) -> p s h q", s=2, h=HPG)
        v_all = region(5).rearrange("p (t d) -> p t d", d=D)
        ksb = sb("ksb", [P, 2, CH])
        st_words = sb("st_words", [P, 2 * KIN * (CH + 1)])
        st = st_words[:, :].rearrange("p (c k t) -> p c k t", c=2, k=KIN)
        xn_t = region(2).rearrange("p (k t) -> p k t", k=KIN)
        xn = region(4).rearrange("p (t d) -> p t d", d=D)
        PARTS_W = KIN * 3 * CH // 2
        tmp = region(3, 2 * PARTS_W + KIN * CH)
        kst = tmp[:, 0:PARTS_W].bitcast(BF16).rearrange("p (a r t) -> p a r t", a=KIN, r=3)
        qst = tmp[:, PARTS_W:2 * PARTS_W].bitcast(BF16).rearrange("p (a r t) -> p a r t", a=KIN, r=3)
        qf = tmp[:, 2 * PARTS_W:].rearrange("p (a t) -> p a t", a=KIN)
        kf = ksb
        qn = st_words[:, 0:2 * CH].rearrange("p (a t) -> p a t", a=2)
        qsq = st_words[:, 2 * CH:4 * CH].rearrange("p (a t) -> p a t", a=2)
        xn_late = x_next = v_all
        hn = region(0).rearrange("p (t d) -> p t d", d=D)
        h_t = region(1).rearrange("p (k t) -> p k t", k=KIN)
        y = hn
        n1 = region(0).rearrange("p (t d) -> p t d", d=D)
        n1_t = region(2).rearrange("p (k t) -> p k t", k=KIN)
        rw = region(3).rearrange("p (k t) -> p k t", k=KIN)
        rt = region(4).rearrange("p (k t) -> p k t", k=KIN)
        r_inv = region(1, KIN * CH).rearrange("p (k t) -> p k t", k=KIN)
        x1 = region(5).rearrange("p (t d) -> p t d", d=D)
        hid = region(3, 2 * R).rearrange("p (a h t) -> p a h t", a=2, h=HT)
        z_relu = ksb

        ps = ctx.enter_context(nc.psum_tensor("ps", [P, 8, CH], F32))
        k_scr = nc.dram_tensor("k_scr", [3, D, S], BF16, kind="Internal").ap()
        q_scr = nc.dram_tensor("q_scr", [3, D, S], BF16, kind="Internal").ap()

        consts_in = sem("consts_in")
        setup_step = sem("setup_step")
        setup_done = sem("setup_done")
        pool_setup = sem("pool_setup")
        x_in = [sem(f"x_in{c}") for c in range(C)]
        x_final = sem("x_final")
        x_out = [sem(f"x_out{c}") for c in range(C)]
        dve = Steps(sem("dve_step"), totals.get("dve", 0))
        pool = Steps(sem("pool_step"), totals.get("pool", 0))
        act_steps = Steps(sem("act_step"), totals.get("act", 0))
        var_ready, rstd_ready, xn_ready = sem("var_ready"), sem("rstd_ready"), sem("xn_ready")
        xt_ps, xt_sb = sem("xt_ps"), sem("xt_sb")
        q_ps, k_ps, v_ps, qt_ps = sem("q_ps"), sem("k_ps"), sem("v_ps"), sem("qt_ps")
        k_read, v_copied, qt_read = sem("k_read"), sem("v_copied"), sem("qt_read")
        v_ready, k_late = sem("v_ready"), sem("k_late")
        k_stored, q_stored = ([sem(f"{x}_stored{kt}") for kt in range(KIN)] for x in "kq")
        q_added, q_ss = sem("q_added"), sem("q_ss")
        ms_ready, ms2_ready, x_moved = sem("ms_ready"), sem("ms2_ready"), sem("x_moved")
        q_sq, q_rn, q_done = sem("q_sq"), sem("q_rn"), sem("q_done")
        k_parts, q_parts = sem("k_parts"), sem("q_parts")
        ops_loaded, k0_loaded, q0_loaded, q0_rest = (
            sem(n) for n in ("ops_loaded", "k0_loaded", "q0_loaded", "q0_rest"))
        qk_ready, exp_done = sem("qk_ready"), sem("exp_done")
        v_slot, pv_done, o_copied = sem("v_slot"), sem("pv_done"), sem("o_copied")
        max_ready, max_free, m_step = sem("max_ready"), sem("max_free"), sem("m_step")
        mrow_ready, mrow_in = sem("mrow_ready"), sem("mrow_in")
        on_ps, hn_ready, ht_ps, ht_sb, y_ps, y_read = (
            sem(n) for n in ("on_ps", "hn_ready", "ht_ps", "ht_sb", "y_ps", "y_read"))
        gate_in, gate_exp, bp_added = sem("gate_in"), sem("gate_exp"), sem("bp_added")
        a_var, a_rstd, rms_ready, n1_ready = (sem(n) for n in ("a_var", "a_rstd", "rms_ready", "n1_ready"))
        nt_ps, nt_sb = sem("nt_ps"), sem("nt_sb")
        kvr_ps, k_copied, r_exp, kv_read = sem("kvr_ps"), sem("k_copied"), sem("r_exp"), sem("kv_read")
        r_guess = sem("r_guess")
        r_den, rw_ready, mix_ps, x2_ready = sem("r_den"), sem("rw_ready"), sem("mix_ps"), sem("x2_ready")
        sq2_done, rms2_ready, n2_ready, mt_ps, mt_sb = (
            sem(n) for n in ("sq2_done", "rms2_ready", "n2_ready", "mt_ps", "mt_sb"))
        fc_relu = sem("fc_relu")
        fc_ps, fc_read, hid_ready, out_ps, out_read = (
            sem(n) for n in ("fc_ps", "fc_read", "hid_ready", "out_ps", "out_read"))
        block = ctx.enter_context(nc.Block())

        NCONST = 24

        def group_loaded(s, hg):
            return 32 * NPROD * (s * (HG - 1) + hg + 1)

        def waited(eng):
            eng.nop(nofuse=True)

        @block.sync
        def _(sp):
            def tiles(w, n):
                return w.rearrange("(k p) n -> p k n", k=n)

            sp.sem_inc(ops_loaded, 32 * NPROD)
            sp.sem_inc(mrow_in, 16)

            def load_x(b):
                xb = io["x"][bass.ds(b, 1), :, :].rearrange("o (t p) d -> p (o t) d", p=P)
                for c in range(C):
                    sp.dma_start(x_next[:, c * TPC:(c + 1) * TPC, :], xb[:, c * TPC:(c + 1) * TPC, :])\
                      .then_inc(x_in[c], 16)

            load_x(0)
            for dst, src in [
                (ident[:, :], io["ident"]),
                (wq[:, :, :], tiles(io["wq_t"], KIN)), (wk[:, :, :], tiles(io["wk_t"], KIN)),
                (wv[:, :, :], tiles(io["wv_t"], KIN)),
                (wprs[:, :, 0:D], tiles(io["wp_t"], KIN)),
                (wprs[:, :, D:D + NGATE], tiles(io["wr_t"], KIN)),
                (wprs[:, :, D + NGATE:NOUT], tiles(io["ws_t"], KIN)),
                (ak[:, :, :], tiles(io["ak_t"], KIN)), (av[:, :, :], tiles(io["av_t"], KIN)),
                (ar[:, :, :], tiles(io["ar_t"], KIN)), (ao[:, :, :], tiles(io["ao_t"], KIN)),
                (wfc[:, :, :], tiles(io["wfc_t"], KIN)), (wmlp[:, :, :], tiles(io["wmlp_t"], HT)),
                (bq[:, :], io["bq"].partition_broadcast(P)), (bv[:, :], io["bv"].partition_broadcast(P)),
                (bp[:, :], io["bp"].partition_broadcast(P)), (embs[:, :], io["emb"].partition_broadcast(P)),
                (brs[:, 0:NGATE], io["br"].partition_broadcast(P)),
                (brs[:, NGATE:NG], io["bs"].partition_broadcast(P)),
                (temp[:, 1, :], io["temp"].partition_broadcast(P)),
                (mixs[:, :], io["mix"].partition_broadcast(P)), (mlps[:, :], io["mlp"].partition_broadcast(P)),
                (bk[:, :], io["bk_cols"]),
                (decay[:, :, :], io["decay_cols"]),
            ]:
                sp.dma_start(dst, src).then_inc(consts_in, 16)

            def load_rows(op, scr, parts, hg, t0, t1, loaded):
                first = (hg % 2) * HPG * S
                for r in range(NPROD):
                    sp.dma_start(
                        op[HD * r:HD * r + HD, first:first + HPG * S].rearrange("d (h t) -> d h t", h=HPG)[:, :, t0:t1],
                        scr[parts[r], hg * HPG * HD:(hg + 1) * HPG * HD, t0:t1].rearrange("(h d) t -> d h t", h=HPG),
                    ).then_inc(loaded, 16)

            def load_operands(hg):
                load_rows(k6, k_scr, K_PART, hg, 0, S, ops_loaded)
                load_rows(q6, q_scr, Q_PART, hg, 0, S, ops_loaded)

            def ffn(s):
                def store_q(c):
                    for kt in range(KIN):
                        sp.wait_ge(q_parts, s * KIN * C + KIN * c + kt + 1)
                        sp.dma_start(q_scr[:, kt * P:(kt + 1) * P, c * CH:(c + 1) * CH].rearrange("r p t -> p r t"),
                                     qst[:, kt, :, :]).then_inc(q_stored[kt], 16)

                def load_k0(c):
                    for stored in k_stored:
                        sp.wait_ge(stored, (s * C + c + 1) * 16)
                    load_rows(k6, k_scr, K_PART, 0, c * CH, (c + 1) * CH, k0_loaded)

                def load_q0(c):
                    for stored in q_stored:
                        sp.wait_ge(stored, (s * C + c + 1) * 16)
                    load_rows(q6, q_scr, Q_PART, 0, c * CH, (c + 1) * CH, q0_loaded if c < C - 1 else q0_rest)

                for c in range(C):
                    if c >= 1:
                        store_q(c - 1)
                        load_k0(c - 1)
                    for kt in range(KIN):
                        if (c, kt) == (C - 1, KIN - 1):
                            sp.wait_ge(k_late, s + 1)
                        else:
                            sp.wait_ge(k_parts, s * (KIN * C - 1) + KIN * c + kt + 1)
                        sp.dma_start(k_scr[:, kt * P:(kt + 1) * P, c * CH:(c + 1) * CH].rearrange("r p t -> p r t"),
                                     kst[:, kt, :, :]).then_inc(k_stored[kt], 16)
                    if c >= 1:
                        load_q0(c - 1)
                load_k0(C - 1)
                store_q(C - 1)
                load_q0(C - 1)
                load_operands(1)

                def load_mrow(ch):
                    sp.wait_ge(mrow_ready, s * NC + ch + 1)
                    rows = q6[ROWS:AUG, :].rearrange("r (g t) -> r g t", t=S)
                    sp.dma_start(rows[:, bass.ds(((ch // C) % 2) * HPG, HPG), bass.ds((ch % C) * CH, CH)],
                                 mrow[:, :]).then_inc(mrow_in, 16)

                load_mrow(0)
                for hg in range(HG):
                    with sp.Fori(0, C if hg < HG - 1 else C - 1) as c:
                        load_mrow(hg * C + c + 1)
                    if hg + 2 < HG:
                        sp.wait_ge(qk_ready, 2 * U * (s * NC + (hg + 1) * C))
                        sp.wait_ge(ops_loaded, group_loaded(s, hg + 1))
                        load_operands(hg + 2)

            with sp.Fori(0, B) as b:
                ob = io["out"][bass.ds(b, 1), :, :].rearrange("o (t p) d -> p (o t) d", p=P)
                for layer in range(2):
                    ffn(b * 2 + layer)
                sp.wait_ge(pv_done, (b + 1) * 2 * NC * U + VSLOTS)
                load_x((b + 1) % B)
                for c in range(C):
                    sp.wait_ge(x_final, b * C + c + 1)
                    sp.dma_start(ob[:, c * TPC:(c + 1) * TPC, :], x_res[:, c * TPC:(c + 1) * TPC, :])\
                      .then_inc(x_out[c], 16)
            for c in range(C):
                sp.wait_ge(x_out[c], (B + 1) * 16)

        @block.gpsimd
        def _(gp):
            gp.memset(ln_shift[:, :], -LN_RANGE * math.log(2.0))
            gp.memset(v_ring[:, :, :, HD:2 * HD], 1.0).then_inc(pool_setup, 1)
            gp.wait_ge(pool_setup, 1)
            gp.memset(k6[ROWS:AUG, :], 1.0).then_inc(pool_setup, 1)
            gp.wait_ge(pool_setup, 2)
            gp.wait_ge(setup_done, 1)

            def ffn(b, s, layer):
                for c in range(C):
                    if layer == 0:
                        gp.wait_ge(xn_ready, s * C + c + 1)
                        gp.wait_ge(x_out[c], (b + 1) * 16)
                        rows = slice(c * TPC, (c + 1) * TPC)
                        gp.tensor_tensor(x_res[:, rows, :], x_next[:, rows, :],
                                         bp[:, :].unsqueeze(1).broadcast_to([P, TPC, D]), ALU.add).then_inc(x_moved, 1)
                    for a in range(KIN - (c == C - 1)):
                        gp.wait_ge(k_read, s * KIN * C + KIN * c + a + 1)
                        pool.did(gp.tensor_tensor(kf[:, a, :], kf[:, a, :], kst[:, a, 0, :], ALU.subtract))
                        pool.wait(gp, b)
                        waited(gp)
                        pool.did(gp.tensor_copy(kst[:, a, 1, :], kf[:, a, :]))
                        pool.wait(gp, b)
                        gp.tensor_tensor(kst[:, a, 2, :], kf[:, a, :], kst[:, a, 1, :], ALU.subtract)\
                          .then_inc(k_parts, 1)
                if layer == 1:
                    gp.wait_ge(xn_ready, (s + 1) * C)
                    gp.tensor_tensor(x_res[:, :, :], x_res[:, :, :],
                                     bp[:, :].unsqueeze(1).broadcast_to([P, KT, D]), ALU.add).then_inc(bp_added, 1)
                for c in range(C):
                    gp.wait_ge(v_copied, s * (KT // 2) + (c + 1) * (TPC // 2))
                    rows = v_all[:, c * TPC:(c + 1) * TPC, :]
                    gp.tensor_tensor(rows, rows, bv[:, :].unsqueeze(1).broadcast_to([P, TPC, D]), ALU.add)\
                      .then_inc(v_ready, 1)
                gp.wait_ge(v_ready, (s + 1) * C)
                waited(gp)

                def v_slots(ch, g0):
                    group = gp.snap((ch // C) * (HPG * HD)) if not isinstance(ch, int) else (ch // C) * HPG * HD
                    for u in range(U):
                        gp.wait_ge(pv_done, g0 + u + 1)
                        waited(gp)
                        gp.tensor_copy(v_ring[:, u % VSLOTS, :, 0:HD],
                                       v_all[:, u, bass.ds(group, HPG * HD)]
                                       .rearrange("p (h d) -> p h d", h=HPG)).then_inc(v_slot, 1)

                with gp.Fori(0, NC) as i:
                    v_slots(i, (s * NC + i) * U)

            with gp.Fori(0, B) as b:
                pool.n = 0
                ffn(b, b * 2, 0)
                for c in range(C):
                    for kt in range(KIN):
                        gp.wait_ge(r_exp, b * KIN * C + KIN * c + kt + 1)
                        waited(gp)
                        r = rt[:, kt, c * CH:(c + 1) * CH]
                        gp.tensor_scalar(r, r, 1.0, 2.0 ** (2 * LN_RANGE), ALU.add, ALU.min).then_inc(r_den, 1)
                ffn(b, b * 2 + 1, 1)
            counts["pool"] = pool.n

        @block.scalar
        def _(act):
            def table_set(n):
                act.add_instruction(mybir.InstLoadActFuncSet(
                    name=nc.get_next_instruction_name(), engine=mybir.EngineType.Activation, ins=[], outs=[],
                    act_func_set_id=n))

            def guess(b, dst, src):
                act_steps.did(act.activation(dst, src, ACT.Ln))
                act_steps.wait(act, b)
                return act.activation(dst, dst, ACT.Exp, scale=-0.5)

            def transposed(b_c, ps_sem, sb_sem, dst, c):
                for kt in range(KIN):
                    act.wait_ge(ps_sem, b_c * KIN + kt + 1)
                    act.copy(dst[:, kt, c * CH:(c + 1) * CH], ps[:, kt, :]).then_inc(sb_sem, 1)

            def ln_guess(b, c, s):
                at = slice(c * TPC, (c + 1) * TPC)
                act.wait_ge(var_ready, s * C + c + 1)
                guess(b, rstd[:, at], var_eps[:, at]).then_inc(rstd_ready, 1)

            def ffn(b, s, layer):
                def parts(c, bank, kind_ps, n0, f, stage, stored, bias, done):
                    for a in range(KIN):
                        act.wait_ge(kind_ps, n0 + a + 1)
                        if c >= 1:
                            act.wait_ge(stored[a], (s * C + c) * 16)
                        act.activation(f[:, a, :], ps[:, bank + a, :], ACT.Identity,
                                       bias=bias[:, a:a + 1] if bias is not None else 0.0)
                        act.activation(stage[:, a, 0, :], ps[:, bank + a, :], ACT.Identity,
                                       bias=bias[:, a:a + 1] if bias is not None else 0.0).then_inc(done, 1)

                transposed(s * C, xt_ps, xt_sb, xn_t, 0)
                for c in range(C):
                    n0 = s * KIN * C + KIN * c
                    for a in range(2):
                        act.wait_ge(q_added, s * 2 * C + 2 * c + a + 1)
                        act.activation(qsq[:, a, :], qn[:, a, :], ACT.Square).then_inc(q_sq, 1)
                    if c + 1 < C:
                        transposed(s * C + c + 1, xt_ps, xt_sb, xn_t, c + 1)
                    act.wait_ge(q_ss, s * C + c + 1)
                    guess(b, rnorm[:, 1, :], rnorm[:, 0, :]).then_inc(q_rn, 1)
                    parts(c, 4, k_ps, n0, kf, kst, k_stored, bk, k_read)
                    parts(c, 6, qt_ps, n0, qf, qst, q_stored, None, qt_read)

                if layer == 0:
                    act.wait_ge(x_moved, (b + 1) * C)
                for i in range(KT // 2):
                    act.wait_ge(v_ps, s * (KT // 2) + i + 1)
                    act.copy(v_all[:, 2 * i:2 * i + 2, :],
                             ps[:, E_BANK + i % 4, :].rearrange("p (t d) -> p t d", t=2)).then_inc(v_copied, 1)

                def exp_unit(n, u):
                    for half in range(2):
                        act.wait_ge(qk_ready, 2 * (n * U + u) + half + 1)
                        if half == 0:
                            act.wait_ge(pv_done, n * U + u - 1 + VSLOTS)
                        act.activation(prob[:, u % 2, 2 * half:2 * half + 2, :],
                                       ps[:, E_BANK + 2 * half:E_BANK + 2 * half + 2, :], ACT.Exp)\
                           .then_inc(exp_done, 1)

                def copy_out(i):
                    act.wait_ge(pv_done, (s * NC + i) * U + U + VSLOTS)
                    act.copy(o_t[:, bass.ds(i * CH, CH)], ps[:, O_BANK, :]).then_inc(o_copied, 1)

                exp_unit(s * NC, 0)
                with act.Fori(0, NC - 1) as i:
                    for u in range(1, U):
                        exp_unit(s * NC + i, u)
                    exp_unit(s * NC + i + 1, 0)
                    copy_out(i)
                for u in range(1, U):
                    exp_unit(s * NC + NC - 1, u)
                copy_out(NC - 1)

                for t in range(KT):
                    if layer == 1:
                        for c in range(C):
                            if t == min(2 * c + 6, KT - 2):
                                ln_guess(b, c, s + 1)
                    if t % 2 == 0:
                        p = t // 2
                        act.wait_ge(ht_ps, s * (KT // 2) + p + 1)
                        act.copy(h_t[:, :, t * P:(t + 2) * P],
                                 ps[:, 2 + p % 2, :].rearrange("p (k t) -> p k t", k=KIN)).then_inc(ht_sb, 1)
                        if p == 0:
                            continue
                    for tt in ((t - 2, t - 1) if t % 2 == 0 else ()):
                        read_y(s, tt)
                        if tt == KT - 4:
                            gates_exp(s, 0)
                for tt in (KT - 2, KT - 1):
                    read_y(s, tt)
                if layer == 1:
                    gates_exp(s, 1)

            def gates_exp(s, part):
                at = slice(part * KT // 2, (part + 1) * KT // 2)
                act.wait_ge(gate_in, 2 * s + part + 1)
                act.activation(lg[:, at, :], lg[:, at, :], ACT.Exp).then_inc(gate_exp, 1)

            def read_y(s, t):
                act.wait_ge(y_ps, s * KT + t + 1)
                act.copy(y[:, t, :], ps[:, 4 + t % 4, 0:D])
                act.copy(lg[:, t, :], ps[:, 4 + t % 4, D:NOUT]).then_inc(y_read, 1)

            table_set(LN_EXP_SET)
            for c in range(C):
                ln_guess(0, c, 0)
            act_steps.before = act_steps.n

            act.wait_ge(setup_step, 2)
            act.activation(temp[:, 2, :], temp[:, 2, :], ACT.Exp, scale=-1.0).then_inc(setup_step, 1)
            act.activation(decay[:, :, :], decay[:, :, :], ACT.Exp).then_inc(setup_step, 1)
            act.wait_ge(setup_step, 5)
            act.activation(decay[:, 0, :], decay[:, 0, :], ACT.Exp, scale=-1.0).then_inc(setup_step, 1)
            table_set(LN_SET)
            act.activation(temp[:, 2, :], temp[:, 2, :], ACT.Ln).then_inc(setup_step, 1)
            table_set(LN_EXP_SET)
            act.wait_ge(setup_done, 1)
            act.sem_inc(exp_done, 2)
            act.sem_inc(pv_done, VSLOTS)
            act.sem_inc(o_copied, 1)
            for c in range(C):
                act.sem_inc(x_out[c], 16)

            with act.Fori(0, B) as b:
                act_steps.n = 0
                ffn(b, b * 2, 0)

                def rms_guess(c, ready, done):
                    at = slice(c * TPC, (c + 1) * TPC)
                    act.wait_ge(ready, b * C + c + 1)
                    guess(b, msq[:, 1, at], msq[:, 0, at]).then_inc(done, 1)

                def seam_guess(c):
                    at = slice(c * TPC, (c + 1) * TPC)
                    act.wait_ge(a_var, b * C + c + 1)
                    guess(b, rstd[:, at], var_eps[:, at]).then_inc(a_rstd, 1)
                    rms_guess(c, ms_ready, rms_ready)

                def squares(c):
                    for t in range(c * TPC, (c + 1) * TPC):
                        act.wait_ge(x2_ready, b * C * 2 + t // 2 + 1)
                        act.activation(n1[:, t, :], x1[:, t, :], ACT.Square, accum_out=msq[:, 0, t:t + 1])\
                           .then_inc(sq2_done, 1)

                seam_guess(0)
                gates_exp(b * 2, 1)
                transposed(b * C, nt_ps, nt_sb, n1_t, 0)
                seam_guess(1)
                for c in range(C):
                    for kt in range(KIN):
                        n = b * KIN * C + KIN * c + kt
                        act.wait_ge(kvr_ps, 2 * n + 1)
                        if c >= 1:
                            act.wait_ge(kv_read, n - KIN + 1)
                        act.copy(ksb[:, kt, :], ps[:, 2 + kt, :]).then_inc(k_copied, 1)
                        act.wait_ge(kvr_ps, 2 * n + 2)
                        act.activation(rt[:, kt, c * CH:(c + 1) * CH], ps[:, 6 + kt, :], ACT.Exp, scale=-1.0)\
                           .then_inc(r_exp, 1)
                    if c + 1 < C:
                        transposed(b * C + c + 1, nt_ps, nt_sb, n1_t, c + 1)
                    for kt in range(KIN):
                        n = b * KIN * C + KIN * c + kt
                        act.wait_ge(r_den, n + 1)
                        if c >= 1:
                            act.wait_ge(rw_ready, n - KIN + 1)
                        act_steps.did(act.activation(r_inv[:, kt, :], rt[:, kt, c * CH:(c + 1) * CH], ACT.Ln,
                                                     scale=2.0 ** -LN_RANGE))
                        act_steps.wait(act, b)
                        act.activation(r_inv[:, kt, :], r_inv[:, kt, :], ACT.Exp, scale=-1.0,
                                       bias=ln_shift[:, :]).then_inc(r_guess, 1)
                    if c + 2 < C:
                        seam_guess(c + 2)
                    if c >= 1:
                        squares(c - 1)
                    if c >= 2:
                        rms_guess(c - 2, ms2_ready, rms2_ready)
                squares(C - 1)
                rms_guess(C - 2, ms2_ready, rms2_ready)
                transposed(b * C, mt_ps, mt_sb, n1_t, 0)
                rms_guess(C - 1, ms2_ready, rms2_ready)

                def square(n):
                    c, j = divmod(n, HT)
                    act.wait_ge(fc_read, b * HT * C + n + 1)
                    if c >= 2:
                        act.wait_ge(out_ps, b * 2 * C + 2 * (c - 1))
                    act.activation(hid[:, c % 2, j, :], z_relu[:, j % 2, :], ACT.Square, scale=0.5)\
                       .then_inc(hid_ready, 1)

                for c in range(C):
                    for j in range(HT):
                        n = HT * c + j
                        act.wait_ge(fc_ps, b * HT * C + n + 1)
                        if n >= 2:
                            act.wait_ge(hid_ready, b * HT * C + n - 1)
                        act.activation(z_relu[:, j % 2, :], ps[:, 2 + j % 4, :], ACT.Relu).then_inc(fc_relu, 1)
                        if n >= 1:
                            square(n - 1)
                        if c >= 2 and j == 1:
                            ln_guess(b, c - 2, b * 2 + 1)
                    if c + 1 < C:
                        transposed(b * C + c + 1, mt_ps, mt_sb, n1_t, c + 1)
                square(HT * C - 1)
                ln_guess(b, C - 2, b * 2 + 1)
                ln_guess(b, C - 1, b * 2 + 1)
                ffn(b, b * 2 + 1, 1)
            counts["act"] = act_steps.n

        @block.vector
        def _(ve):
            def link(ins, b):
                dve.did(ins)
                dve.wait(ve, b)

            def statistics(b, src, c, signal):
                tiles = range(c * TPC, (c + 1) * TPC)
                ready = [dve.did(ve.bn_stats(bn[:, t, :], src[:, t, :])) for t in tiles]
                for t, done in zip(tiles, ready):
                    dve.wait(ve, b, done)
                    waited(ve)
                    ins = ve.bn_aggr(mv[:, t, :], bn[:, t, :])
                link(ins, b)
                at = slice(c * TPC, (c + 1) * TPC)
                ve.tensor_scalar(var_eps[:, at], mv[:, at, 1], LN_EPS, None, ALU.add).then_inc(signal, 1)

            def normalise(b, src, dst, c, s):
                at = slice(c * TPC, (c + 1) * TPC)
                ve.wait_ge(rstd_ready, s * C + c + 1)
                refine(b, rstd[:, at], var_eps[:, at], newton[:, 0:TPC])
                for t in range(c * TPC, (c + 1) * TPC):
                    last = ve.tensor_scalar(dst[:, t, :], src[:, t, :], mv[:, t, 0:1], rstd[:, t:t + 1],
                                            ALU.subtract, ALU.mult)
                last.then_inc(xn_ready, 1)

            def refine(b, y, x, tmp):
                link(ve.tensor_tensor(tmp, x, y, ALU.mult), b)
                link(ve.tensor_tensor(tmp, tmp, y, ALU.mult), b)
                link(ve.tensor_scalar(tmp, tmp, -0.5, 1.5, ALU.mult, ALU.add), b)
                link(ve.tensor_tensor(y, y, tmp, ALU.mult), b)

            def heads(ap, t):
                return ap.rearrange("p (t h d) -> p t h d", t=t, h=H)

            def ffn(b, s, layer):
                def cut_q(c, a):
                    ve.wait_ge(qt_read, s * KIN * C + KIN * c + a + 1)
                    link(ve.tensor_tensor(qf[:, a, :], qf[:, a, :], qst[:, a, 0, :], ALU.subtract), b)
                    link(ve.tensor_copy(qst[:, a, 1, :], qf[:, a, :]), b)
                    ve.tensor_tensor(qst[:, a, 2, :], qf[:, a, :], qst[:, a, 1, :], ALU.subtract).then_inc(q_parts, 1)

                for c in range(C):
                    for a in range(2):
                        n = s * 2 * C + 2 * c + a
                        ve.wait_ge(q_ps, n + 1)
                        if c >= 1:
                            ve.wait_ge(qt_ps, s * KIN * C + KIN * c)
                        ve.tensor_tensor(qn[:, a, :].rearrange("p (t d) -> p t d", t=2),
                                         ps[:, 2 + a, :].rearrange("p (t d) -> p t d", t=2),
                                         bq[:, :].unsqueeze(1).broadcast_to([P, 2, D]), ALU.add).then_inc(q_added, 1)
                    if c >= 1:
                        cut_q(c - 1, 0)
                    for a in range(2):
                        ve.wait_ge(q_sq, s * 2 * C + 2 * c + a + 1)
                        last = ve.tensor_reduce(rnorm[:, 0, a * 2 * H:(a + 1) * 2 * H].rearrange("p (t h) -> p t h", t=2),
                                                heads(qsq[:, a, :], 2), AX.X, ALU.add)
                    last.then_inc(q_ss, 1)
                    if c >= 1:
                        cut_q(c - 1, 1)
                    ve.wait_ge(q_rn, s * C + c + 1)
                    refine(b, rnorm[:, 1, :], rnorm[:, 0, :], newton[:, :])
                    by_head = rnorm[:, 1, :].rearrange("p (t h) -> p t h", h=H)
                    link(ve.tensor_tensor(by_head, by_head, temp[:, 0:1, :].broadcast_to([P, TPC, H]), ALU.mult), b)
                    for a in range(2):
                        scale = rnorm[:, 1, a * 2 * H:(a + 1) * 2 * H].rearrange("p (t h) -> p t h", t=2).unsqueeze(3)\
                            .broadcast_to([P, 2, H, HD])
                        k1 = dve.did(ve.tensor_tensor(heads(qn[:, a, :], 2), heads(qn[:, a, :], 2), scale, ALU.mult))
                        dve.wait(ve, b, k1)
                        v2 = qn[:, a, :].rearrange("p (t d) -> p t d", t=2)
                        ve.tensor_tensor(v2, v2, embs[:, :].unsqueeze(1).broadcast_to([P, 2, D]), ALU.add)\
                          .then_inc(q_done, 1)
                    if c == C - 1:
                        a = KIN - 1
                        ve.wait_ge(k_read, (s + 1) * KIN * C)
                        link(ve.tensor_tensor(kf[:, a, :], kf[:, a, :], kst[:, a, 0, :], ALU.subtract), b)
                        link(ve.tensor_copy(kst[:, a, 1, :], kf[:, a, :]), b)
                        ve.tensor_tensor(kst[:, a, 2, :], kf[:, a, :], kst[:, a, 1, :], ALU.subtract)\
                          .then_inc(k_late, 1)
                cut_q(C - 1, 0)
                cut_q(C - 1, 1)

                def elements(base, count, mt, n, tile, turn=0):
                    split = []
                    for e in range(count):
                        bank = M_BANK + (e + turn) % M_BANKS
                        ve.wait_ge(max_ready, base + e + 1)
                        if e == mt:
                            ve.wait_ge(mrow_in, 16 * (n + 1))
                            ve.tensor_copy(mrow[:, :], ps[0:3 * HPG, bank, 0:CH // 2].bitcast(BF16))\
                              .then_inc(mrow_ready, 1)
                            ve.wait_ge(mrow_ready, n + 1)
                            ve.sem_inc(max_free, 1)
                            continue
                        ve.tensor_reduce(pmax[:, tile:tile + 1], ps[:, bank, :], AX.X, ALU.max).then_inc(max_free, 1)
                        tile += 1
                        if tile == HPG * TPC * C:
                            ve.wait_ge(max_free, base + e + 1)
                            ve.tensor_reduce(negm[:, 0, :], pmax[:, :].rearrange("p (x c) -> p x c", c=C), AX.X,
                                             ALU.max, negate=True).then_inc(m_step, 1)
                            ve.wait_ge(m_step, 5 * n + 1)
                            split = [0, 1, 2, 3]
                            tile = 0
                        elif split:
                            split_max(n, split.pop(0))

                def split_max(n, step):
                    parts = mparts[:, :].rearrange("p (q r h) -> p r h q", r=3, h=HPG)
                    neg = [negm[:, j, :].rearrange("p (h q) -> p h q", h=HPG) for j in range(2)]
                    ve.wait_ge(m_step, 5 * n + 1 + step)
                    if step == 0:
                        ve.tensor_copy(parts[:, 0, :, :], neg[0]).then_inc(m_step, 1)
                    if step == 1:
                        ve.tensor_tensor(neg[1], neg[0], parts[:, 0, :, :], ALU.subtract).then_inc(m_step, 1)
                    if step == 2:
                        ve.tensor_copy(parts[:, 1, :, :], neg[1]).then_inc(m_step, 1)
                    if step == 3:
                        ve.tensor_tensor(parts[:, 2, :, :], neg[1], parts[:, 1, :, :], ALU.subtract).then_inc(m_step, 1)

                elements(s * RING_STAGE, RING_PRO, MT_PRO, s * NC, 0, RING_TURN)
                with ve.Fori(0, NC - 1) as i:
                    elements(s * RING_STAGE + RING_PRO + i * RING_BODY, RING_BODY, MT_BODY, s * NC + i + 1, 4 * LEAD)

                for t in range(KT):
                    ve.wait_ge(on_ps, s * KT + t + 1)
                    o = ps[:, t % 2, :].rearrange("p (h e) -> p h e", h=H)
                    k1 = dve.did(ve.reciprocal(rden[:, t, :].unsqueeze(2), o[:, :, HD:HD + 1]))
                    dve.wait(ve, b, k1)
                    ve.tensor_tensor(hn[:, t, :].rearrange("p (h d) -> p h d", h=H), o[:, :, 0:HD],
                                     rden[:, t, :].unsqueeze(2).broadcast_to([P, H, HD]), ALU.mult)\
                      .then_inc(hn_ready, 1)
                    for c in range(C if layer == 1 else 0):
                        if t == 2 * c + 3:
                            ve.wait_ge(x_in[c], (b + 2) * 16)
                            statistics(b, x_next, c, var_ready)
                        if t == min(2 * c + 7, KT - 1):
                            normalise(b, x_next, xn, c, s + 1)
                def gates(part):
                    at = slice(part * KT // 2, (part + 1) * KT // 2)
                    ve.wait_ge(y_read, s * KT + (part + 1) * KT // 2)
                    routed, shared = lg[:, at, 0:NGATE], lg[:, at, NGATE:NG]
                    col = [gsm[:, j, at].unsqueeze(2) for j in range(8)]
                    link(ve.tensor_tensor(lg[:, at, :], lg[:, at, :],
                                          brs[:, :].unsqueeze(1).broadcast_to([P, KT // 2, NG]), ALU.add), b)
                    ve.tensor_reduce(col[0], routed, AX.X, ALU.max)
                    link(ve.tensor_reduce(col[1], shared, AX.X, ALU.max), b)
                    link(ve.tensor_tensor(routed, routed, col[0].broadcast_to([P, KT // 2, NGATE]), ALU.subtract), b)
                    ve.tensor_tensor(shared, shared, col[1].broadcast_to([P, KT // 2, NSH]), ALU.subtract).then_inc(gate_in, 1)
                    ve.wait_ge(gate_exp, 2 * s + part + 1)
                    link(ve.tensor_reduce(col[2], routed, AX.X, ALU.add), b)
                    dve.did(ve.tensor_reduce(col[3], shared, AX.X, ALU.add))
                    for t in range(part * KT // 2, (part + 1) * KT // 2):
                        last = ve.max(top[:, t, :], lg[:, t, 0:NGATE])
                    link(last, b)
                    link(ve.tensor_reduce(col[4], top[:, at, 0:TOPK], AX.X, ALU.add), b)
                    link(ve.reciprocal(gsm[:, 2:4, at], gsm[:, 2:4, at]), b)
                    link(ve.tensor_tensor(col[4], col[4], col[2], ALU.mult), b)
                    link(ve.tensor_tensor(sw[:, at, :], shared, col[3].broadcast_to([P, KT // 2, NSH]), ALU.mult), b)
                    link(ve.tensor_tensor(col[5], sw[:, at, 0:1], sw[:, at, 1:2], ALU.add), b)
                    link(ve.tensor_tensor(col[5], col[5], sw[:, at, 0:1], ALU.mult), b)
                    link(ve.scalar_tensor_tensor(col[6], col[4], float(TOPK), sw[:, at, 1:2], ALU.mult, ALU.mult), b)
                    link(ve.tensor_tensor(col[7], col[5], col[6], ALU.add), b)

                if layer == 1:
                    ve.wait_ge(bp_added, b + 1)

                def residual(c):
                    for t in range(c * TPC, (c + 1) * TPC):
                        last = ve.scalar_tensor_tensor(x_res[:, t, :], y[:, t, :], gsm[:, 7, t:t + 1], x_res[:, t, :],
                                                       ALU.mult, ALU.add)
                    return last

                gates(0)
                if layer == 1:
                    for c in range(C):
                        if c == C // 2:
                            gates(1)
                        residual(c).then_inc(x_final, 1)
                    ve.wait_ge(x_final, (b + 1) * C)
                return gates, residual

            def rms(b, c, x, dst, count, guessed, signal):
                at = slice(c * TPC, (c + 1) * TPC)
                ve.wait_ge(guessed, count)
                refine(b, msq[:, 1, at], msq[:, 0, at], newton[:, 0:TPC])
                for t in range(c * TPC, (c + 1) * TPC):
                    last = ve.tensor_scalar(dst[:, t, :], x[:, t, :], msq[:, 1, t:t + 1], None, ALU.mult)
                last.then_inc(signal, 1)

            def recurrence(b, gates, residual):
                def seam(c):
                    at = slice(c * TPC, (c + 1) * TPC)
                    link(residual(c), b)
                    statistics(b, x_res, c, a_var)
                    ve.wait_ge(a_rstd, b * C + c + 1)
                    refine(b, rstd[:, at], var_eps[:, at], newton[:, 0:TPC])
                    link(ve.tensor_tensor(msq[:, 0, at], mv[:, at, 1], rstd[:, at], ALU.mult), b)
                    link(ve.tensor_tensor(msq[:, 0, at], msq[:, 0, at], rstd[:, at], ALU.mult), b)
                    ve.tensor_scalar(msq[:, 0, at], msq[:, 0, at], RMS_EPS, None, ALU.add).then_inc(ms_ready, 1)
                    for t in range(c * TPC, (c + 1) * TPC):
                        last = ve.tensor_scalar(x1[:, t, :], x_res[:, t, :], mv[:, t, 0:1], rstd[:, t:t + 1],
                                                ALU.subtract, ALU.mult)
                    dve.did(last)
                    rms(b, c, x1, n1, b * C + c + 1, rms_ready, n1_ready)

                def second_norm(c):
                    at = slice(c * TPC, (c + 1) * TPC)
                    ve.wait_ge(sq2_done, b * KT + (c + 1) * TPC)
                    ve.tensor_scalar(msq[:, 0, at], msq[:, 0, at], 1.0 / D, RMS_EPS, ALU.mult, ALU.add)\
                      .then_inc(ms2_ready, 1)
                    rms(b, c, x1, n1, b * C + c + 1, rms2_ready, n2_ready)

                seam(0)
                gates(1)
                seam(1)

                def add_mix(c):
                    for a in range(2):
                        ve.wait_ge(mix_ps, b * 2 * C + 2 * c + a + 1)
                        x = x1[:, c * TPC + 2 * a:c * TPC + 2 * a + 2, :]
                        ve.tensor_tensor(x, x, ps[:, a, :].rearrange("p (t d) -> p t d", t=2), ALU.add)\
                          .then_inc(x2_ready, 1)

                for c in range(C):
                    span = slice(c * CH, (c + 1) * CH)
                    kv = [rw[:, kt, span] for kt in range(KIN)]
                    for kt in range(KIN):
                        n = b * KIN * C + KIN * c + kt
                        ve.wait_ge(k_copied, n + 1)
                        dve.did(ve.tensor_tensor(kv[kt], ps[:, 4 + kt, :], ksb[:, kt, :], ALU.mult))
                        dve.wait(ve, b)
                        if c >= 1:
                            dve.did(ve.tensor_copy(st[:, c % 2, kt, 0:1], st[:, (c - 1) % 2, kt, CH:CH + 1]))
                        else:
                            dve.did(ve.memset(st[:, 0, kt, 0:1], 0.0))
                        dve.wait(ve, b)
                        dve.did(ve.tensor_tensor_scan(st[:, c % 2, kt, 1:CH + 1],
                                                      decay[:, 0, kt:kt + 1].broadcast_to([P, CH]), kv[kt],
                                                      st[:, c % 2, kt, 0:1], ALU.mult, ALU.add))
                        dve.wait(ve, b)
                        ve.scalar_tensor_tensor(kv[kt], kv[kt], decay[:, 1, kt:kt + 1], st[:, c % 2, kt, 0:CH],
                                                ALU.mult, ALU.add).then_inc(kv_read, 1)
                    for kt in range(KIN):
                        n = b * KIN * C + KIN * c + kt
                        ve.wait_ge(r_guess, n + 1)
                        d, y = rt[:, kt, span], r_inv[:, kt, :]
                        dve.did(ve.tensor_tensor(d, d, y, ALU.mult))
                        dve.wait(ve, b)
                        dve.did(ve.scalar_tensor_tensor(y, d, 2.0, y, ALU.subtract, ALU.mult))
                        dve.wait(ve, b)
                        ve.wait_ge(kv_read, n + 1)
                        ve.scalar_tensor_tensor(kv[kt], kv[kt], -1.0, y, ALU.mult, ALU.mult).then_inc(rw_ready, 1)
                    if c >= 1:
                        add_mix(c - 1)
                    if c + 2 < C:
                        seam(c + 2)
                    if c >= 2:
                        second_norm(c - 2)
                add_mix(C - 1)
                second_norm(C - 2)
                second_norm(C - 1)

                def add_out(c):
                    for a in range(2):
                        ve.wait_ge(out_ps, b * 2 * C + 2 * c + a + 1)
                        x = x_res[:, c * TPC + 2 * a:c * TPC + 2 * a + 2, :]
                        dve.wait(ve, b)
                        ve.tensor_tensor(x, x, ps[:, 6 + a, :].rearrange("p (t d) -> p t d", t=2), ALU.add)\
                          .then_inc(out_read, 1)
                    ve.wait_ge(out_read, b * 2 * C + 2 * c + 2)
                    statistics(b, x_res, c, var_ready)

                for c in range(C):
                    xs = x_res[:, c * TPC:(c + 1) * TPC, :]
                    dve.did(ve.tensor_tensor(xs, xs, x1[:, c * TPC:(c + 1) * TPC, :], ALU.add))
                    for j in range(HT):
                        ve.wait_ge(fc_relu, b * HT * C + HT * c + j + 1)
                        ve.tensor_tensor(z_relu[:, j % 2, :], z_relu[:, j % 2, :], ps[:, 2 + j % 4, :], ALU.add)\
                          .then_inc(fc_read, 1)
                        if c >= 2 and j == 3:
                            normalise(b, x_res, xn_late, c - 2, b * 2 + 1)
                    if c >= 1:
                        add_out(c - 1)
                add_out(C - 1)
                normalise(b, x_res, xn_late, C - 2, b * 2 + 1)
                normalise(b, x_res, xn_late, C - 1, b * 2 + 1)

            for c in range(C):
                ve.wait_ge(x_in[c], 16)
                statistics(0, x_next, c, var_ready)
                normalise(0, x_next, xn, c, 0)
            dve.before = dve.n

            ve.wait_ge(consts_in, 16 * NCONST)
            ve.wait_ge(pool_setup, 2)
            ve.tensor_copy(ident_bf[:, :], ident[:, :])
            ve.tensor_scalar(temp[:, 3, :], temp[:, 1, :], -1.0, None, ALU.mult).then_inc(setup_step, 1)
            ve.wait_ge(setup_step, 1)
            ve.tensor_tensor(temp[:, 2, :], temp[:, 1, :], temp[:, 3, :], ALU.max).then_inc(setup_step, 1)
            ve.tensor_tensor(ao[:, :, :], ao[:, :, :], mixs[:, :].unsqueeze(1).broadcast_to([P, KIN, D]), ALU.mult)
            ve.tensor_tensor(wmlp[:, :, :], wmlp[:, :, :], mlps[:, :].unsqueeze(1).broadcast_to([P, HT, D]), ALU.mult)
            ve.tensor_scalar(bp[:, :], bp[:, :], 0.5, None, ALU.mult)
            ve.wait_ge(setup_step, 4)
            ve.tensor_scalar(temp[:, 2, :], temp[:, 2, :], 1.0, None, ALU.add).then_inc(setup_step, 1)
            ve.wait_ge(setup_step, 7)
            ve.scalar_tensor_tensor(temp[:, 0, :], temp[:, 1, :], 0.0, temp[:, 2, :], ALU.max, ALU.add)\
              .then_inc(setup_step, 1)
            ve.wait_ge(setup_step, 8)
            ve.tensor_scalar(temp[:, 0, :], temp[:, 0, :], HD ** -0.5, None, ALU.mult).then_inc(setup_step, 1)
            ve.wait_ge(setup_step, 9)
            ve.tensor_tensor(embs[:, :].rearrange("p (h d) -> p h d", h=H), embs[:, :].rearrange("p (h d) -> p h d", h=H),
                             temp[:, 0, :].unsqueeze(2).broadcast_to([P, H, HD]), ALU.mult).then_inc(setup_step, 1)
            ve.wait_ge(setup_step, 10)
            ve.memset(st[:, :, :, 0:1], 0.0).then_inc(setup_done, 1)

            with ve.Fori(0, B) as b:
                dve.n = 0
                recurrence(b, *ffn(b, b * 2, 0))
                ffn(b, b * 2 + 1, 1)
            counts["dve"] = dve.n

        @block.tensor
        def _(pe):
            pe.wait_ge(setup_done, 1)

            def transposes(c, src, ready, ready_at, signal, banks=(0, 1)):
                pe.wait_ge(ready, ready_at)
                for kt in range(KIN):
                    for j in range(TPC):
                        last = pe.transpose(ps[:, banks[kt], j * P:(j + 1) * P],
                                            src[:, c * TPC + j, kt * P:(kt + 1) * P], ident[:, :])
                    last.then_inc(signal, 1)

            def natural(c, a, w, acts, bank, signal):
                for j in range(2):
                    t = c * TPC + 2 * a + j
                    for kt in range(KIN):
                        last = pe.matmul(ps[:, bank, j * D:(j + 1) * D], acts[:, kt, t * P:(t + 1) * P], w[:, kt, :],
                                         start=kt == 0, stop=kt == KIN - 1)
                last.then_inc(signal, 1)

            def columns(c, m, w, acts, bank):
                for kt in range(KIN):
                    last = pe.matmul(ps[:, bank, :], w[:, kt, m * P:(m + 1) * P], acts[:, kt, c * CH:(c + 1) * CH],
                                     start=kt == 0, stop=kt == KIN - 1)
                return last

            def ffn(b, s, layer):
                normed = xn_late if layer == 1 else xn
                transposes(0, normed, xn_ready, s * C + 1, xt_ps)
                if layer == 1:
                    pe.wait_ge(fc_read, (b + 1) * HT * C)
                    pe.wait_ge(out_read, (b + 1) * 2 * C)
                def queries(c):
                    n = s * 2 * C + 2 * c
                    pe.wait_ge(xt_sb, n + 2)
                    for a in range(2):
                        if c >= 1:
                            pe.wait_ge(q_added, n - 2 + a + 1)
                        natural(c, a, wq, xn_t, 2 + a, q_ps)

                queries(0)
                for c in range(C):
                    n = s * 2 * C + 2 * c
                    if c + 1 < C:
                        transposes(c + 1, normed, xn_ready, s * C + c + 2, xt_ps)
                    for a in range(KIN):
                        if c >= 1:
                            pe.wait_ge(k_read, n - 2 + a + 1)
                        columns(c, a, wk, xn_t, 4 + a).then_inc(k_ps, 1)
                    if c + 1 < C:
                        queries(c + 1)
                    pe.wait_ge(q_done, n + 2)
                    if c >= 1:
                        pe.wait_ge(qt_read, n)
                    for kt in range(KIN):
                        for j in range(TPC):
                            a, t = divmod(j, 2)
                            last = pe.transpose(ps[:, 6 + kt, j * P:(j + 1) * P],
                                                qn[:, a, t * D + kt * P:t * D + (kt + 1) * P], ident[:, :])
                        last.then_inc(qt_ps, 1)

                n = (s + 1) * 2 * C
                for sm in (qt_read, k_read):
                    pe.wait_ge(sm, n)

                def values(t):
                    if t >= 8:
                        pe.wait_ge(v_copied, s * (KT // 2) + t // 2 - 3)
                    for kt in range(KIN):
                        last = pe.matmul(ps[:, E_BANK + (t // 2) % 4, t % 2 * D:(t % 2 + 1) * D],
                                         xn_t[:, kt, t * P:(t + 1) * P], wv[:, kt, :], start=kt == 0, stop=kt == KIN - 1)
                    if t % 2 == 1:
                        last.then_inc(v_ps, 1)

                def offsets(ch):
                    at_k = ((ch // C) % 2) * (HPG * S)
                    at_q = at_k + (ch % C) * CH
                    return (at_k, at_q) if isinstance(ch, int) else (pe.snap(at_k), pe.snap(at_q))

                def scores(at, u, half, n):
                    pe.wait_ge(exp_done, 2 * (n * U + u) + half + 1)
                    for h in (2 * half, 2 * half + 1):
                        last = pe.matmul(ps[:, E_BANK + h, :], k6[0:AUG, bass.ds(at[0] + h * S + u * P, P)],
                                         q6[0:AUG, bass.ds(at[1] + h * S, CH)], start=True, stop=True)
                    last.then_inc(qk_ready, 1)

                def element(base, e, mt, m_at, at, tile, turn=0):
                    back = e - M_BANKS + 1 if e >= M_BANKS else -((RING_BODY - 1 - e) % M_BANKS)
                    if not (mt == MT_PRO and e < M_BANKS):
                        pe.wait_ge(max_free, base + back)
                    bank = M_BANK + (e + turn) % M_BANKS
                    if e == mt:
                        pe.wait_ge(m_step, 5 * m_at + 5)
                        waited(pe)
                        for x in range(TPC):
                            last = pe.transpose(ps[0:3 * HPG, bank, x * P // 2:(x + 1) * P // 2].bitcast(BF16),
                                                mparts[:, x * 3 * HPG:(x + 1) * 3 * HPG], ident_bf[:, :])
                        last.then_inc(max_ready, 1)
                        return
                    x, kc = divmod(tile, C)
                    h, qt = divmod(x, TPC)
                    pe.matmul(ps[:, bank, :], q6[0:ROWS, bass.ds(at[1] + h * S + qt * P, P)],
                              k6[0:ROWS, bass.ds(at[0] + h * S + kc * CH, CH)], start=True, stop=True)\
                      .then_inc(max_ready, 1)

                def products(u, n):
                    pe.wait_ge(exp_done, 2 * (n * U + u) + 4)
                    pe.wait_ge(v_slot, n * U + u + 1)
                    if u == 0:
                        pe.wait_ge(o_copied, n + 1)
                    for h in range(HPG):
                        last = pe.matmul(ps[32 * h:32 * h + 2 * HD, O_BANK, :], v_ring[:, u % VSLOTS, h, :],
                                         prob[:, u % 2, h, :], start=u == 0, stop=u == U - 1)
                    last.then_inc(pv_done, 1)

                NT = HPG * TPC * C
                pe.wait_ge(k0_loaded, 16 * NPROD * (s + 1) * C)
                pe.wait_ge(q0_loaded, 16 * NPROD * (s + 1) * (C - 1))
                at0, at1 = offsets(0), offsets(1)
                tile = 0
                for e in range(RING_PRO):
                    first = e < NT
                    if e == NT:
                        pe.wait_ge(q0_rest, 16 * NPROD * (s + 1))
                    element(s * RING_STAGE, e, MT_PRO, s * NC, at0 if first else at1, tile % NT, RING_TURN)
                    tile += e != MT_PRO
                    if e % 4 == 3 and e // 4 < KT:
                        values(e // 4)
                pe.wait_ge(mrow_in, 16 * (s * NC + 2))
                pe.wait_ge(v_copied, (s + 1) * (KT // 2))
                for half in range(2):
                    scores(at0, 0, half, s * NC)

                with pe.Fori(0, NC - 1) as i:
                    n = s * NC + i
                    here, ahead, ahead2 = offsets(i), offsets(i + 1), offsets((i + 2) % NC)
                    base = s * RING_STAGE + RING_PRO + i * RING_BODY
                    tile, e = 4 * LEAD, 0

                    def elements(count):
                        nonlocal tile, e
                        for _ in range(count):
                            if tile == NT:
                                pe.wait_ge(ops_loaded, group_loaded(s, ((i + 2) % NC) // C))
                            element(base, e, MT_BODY, n + 1, ahead if tile < NT else ahead2, tile % NT)
                            tile += e != MT_BODY
                            e += 1

                    for u in range(U):
                        if u == U - 1:
                            pe.wait_ge(mrow_in, 16 * (n + 3))
                        elements(1)
                        for half in range(2):
                            if u < U - 1:
                                scores(here, u + 1, half, n)
                            else:
                                scores(ahead, 0, half, n + 1)
                            elements(1 + half + (u == U - 1 and half == 1))
                        products(u, n)
                n = s * NC + NC - 1
                at = offsets(NC - 1)
                for u in range(U):
                    if u < U - 1:
                        for half in range(2):
                            scores(at, u + 1, half, n)
                    products(u, n)

                pe.wait_ge(o_copied, (s + 1) * NC + 1)
                pe.wait_ge(max_free, (s + 1) * RING_STAGE)

                def turn(t):
                    if t >= 2:
                        pe.wait_ge(hn_ready, s * KT + t - 1)
                    for hg in range(HG):
                        last = pe.transpose(ps[:, t % 2, hg * P:(hg + 1) * P], o_t[:, hg * S + t * P:hg * S + (t + 1) * P],
                                            ident[:, :])
                    last.then_inc(on_ps, 1)

                def back(p):
                    pe.wait_ge(hn_ready, s * KT + 2 * p + 2)
                    if p >= 2:
                        pe.wait_ge(ht_sb, s * (KT // 2) + p - 1)
                    for j in range(2):
                        for kt in range(KIN):
                            last = pe.transpose(ps[:, 2 + p % 2, kt * 2 * P + j * P:kt * 2 * P + (j + 1) * P],
                                                hn[:, 2 * p + j, kt * P:(kt + 1) * P], ident[:, :])
                    last.then_inc(ht_ps, 1)

                def project(t):
                    pe.wait_ge(ht_sb, s * (KT // 2) + t // 2 + 1)
                    if t >= 4:
                        pe.wait_ge(y_read, s * KT + t - 3)
                    for kt in range(KIN):
                        last = pe.matmul(ps[:, 4 + t % 4, 0:NOUT], h_t[:, kt, t * P:(t + 1) * P], wprs[:, kt, :],
                                         start=kt == 0, stop=kt == KIN - 1)
                    last.then_inc(y_ps, 1)

                turn(0)
                turn(1)
                for p in range(KT // 2):
                    if 2 * p + 2 < KT:
                        turn(2 * p + 2)
                        turn(2 * p + 3)
                    back(p)
                    if p >= 1:
                        project(2 * p - 2)
                        project(2 * p - 1)
                project(KT - 2)
                project(KT - 1)
                pe.wait_ge(y_read, (s + 1) * KT)

            def recurrence(b):
                transposes(0, n1, n1_ready, b * C + 1, nt_ps)

                def mix(c):
                    pe.wait_ge(rw_ready, b * KIN * C + KIN * (c + 1))
                    if c + 2 < C:
                        pe.wait_ge(nt_sb, b * KIN * C + KIN * (c + 3))
                    else:
                        pe.wait_ge(nt_sb, (b + 1) * KIN * C)
                    for a in range(2):
                        if c >= 1:
                            pe.wait_ge(x2_ready, b * 2 * C + 2 * (c - 1) + a + 1)
                        natural(c, a, ao, rw, a, mix_ps)

                for c in range(C):
                    n = b * KIN * C + KIN * c
                    pe.wait_ge(nt_sb, n + KIN)
                    for kt in range(KIN):
                        if c >= 1:
                            pe.wait_ge(kv_read, n - KIN + kt + 1)
                            pe.wait_ge(r_exp, n - KIN + kt + 1)
                        columns(c, kt, ak, n1_t, 2 + kt)
                        columns(c, kt, av, n1_t, 4 + kt).then_inc(kvr_ps, 1)
                        columns(c, kt, ar, n1_t, 6 + kt).then_inc(kvr_ps, 1)
                    if c + 1 < C:
                        if c >= 2:
                            pe.wait_ge(x2_ready, b * 2 * C + 2 * (c - 1))
                        transposes(c + 1, n1, n1_ready, b * C + c + 2, nt_ps)
                    if c >= 1:
                        mix(c - 1)
                mix(C - 1)
                pe.wait_ge(x2_ready, (b + 1) * 2 * C)
                transposes(0, n1, n2_ready, b * C + 1, mt_ps)

                def down(c):
                    pe.wait_ge(hid_ready, b * HT * C + HT * (c + 1))
                    for a in range(2):
                        if c >= 1:
                            pe.wait_ge(out_read, b * 2 * C + 2 * (c - 1) + a + 1)
                        for j in range(2):
                            t = 2 * a + j
                            for m in range(HT):
                                last = pe.matmul(ps[:, 6 + a, j * D:(j + 1) * D], hid[:, c % 2, m, t * P:(t + 1) * P],
                                                 wmlp[:, m, :], start=m == 0, stop=m == HT - 1)
                        last.then_inc(out_ps, 1)

                for c in range(C):
                    pe.wait_ge(mt_sb, b * KIN * C + KIN * (c + 1))
                    for m in range(HT):
                        n = HT * c + m
                        if n >= 4:
                            pe.wait_ge(fc_read, b * HT * C + n - 3)
                        columns(c, m, wfc, n1_t, 2 + m % 4).then_inc(fc_ps, 1)
                    if c + 1 < C:
                        transposes(c + 1, n1, n2_ready, b * C + c + 2, mt_ps)
                    if c >= 1:
                        down(c - 1)
                down(C - 1)

            with pe.Fori(0, B) as b:
                ffn(b, b * 2, 0)
                recurrence(b)
                ffn(b, b * 2 + 1, 1)
    return counts


def kernel(**inputs):
    import numpy as np
    import concourse.bacc as bacc
    from concourse import mybir as _mybir
    from concourse.bass_utils import run_bass_kernel_spmd as _run

    def arr(name):
        return np.asarray(inputs[name])

    def turned(name):
        return np.ascontiguousarray(arr(name).T)

    def columns_of(*names):
        return np.ascontiguousarray(np.stack([arr(n).reshape(2, 128).T for n in names], axis=1))

    host = {
        "x": np.ascontiguousarray(arr("L0_attn_x")),
        "ident": np.eye(128, dtype=np.float32),
        "wq_t": turned("L0_ffn_Wq"), "wk_t": turned("L0_ffn_Wk"), "wv_t": turned("L0_ffn_Wv"),
        "wp_t": turned("L0_ffn_Wp"), "wr_t": turned("L0_ffn_Wr"), "ws_t": turned("L0_ffn_Ws"),
        "ak_t": turned("L0_attn_Wk"), "av_t": turned("L0_attn_Wv"), "ar_t": turned("L0_attn_Wr"),
        "ao_t": turned("L0_attn_Wo"), "wfc_t": turned("L0_attn_Wfc"), "wmlp_t": turned("L0_attn_Wmlp"),
        "bq": arr("L0_ffn_bq"), "bv": arr("L0_ffn_bv"), "bp": arr("L0_ffn_bp"),
        "br": arr("L0_ffn_br"), "bs": arr("L0_ffn_bs"),
        "emb": np.ascontiguousarray(arr("L0_ffn_query_embedding").reshape(-1)),
        "temp": np.ascontiguousarray(arr("L0_ffn_temperature").reshape(-1)),
        "mix": arr("L0_attn_mixer_scale"), "mlp": arr("L0_attn_mlp_scale"),
        "bk_cols": np.ascontiguousarray(arr("L0_ffn_bk").reshape(2, 128).T),
        "decay_cols": columns_of("L0_attn_time_decay", "L0_attn_time_first"),
    }
    B, S, _ = host["x"].shape

    def program(totals):
        nc = bacc.Bacc("TRN2", target_bir_lowering=False, num_devices=1)
        io = {n: nc.dram_tensor(f"in_{n}", a.shape, _mybir.dt.from_np(a.dtype), kind="ExternalInput").ap()
              for n, a in host.items()}
        io["out"] = nc.dram_tensor("out_0", host["x"].shape, _mybir.dt.float32, kind="ExternalOutput").ap()
        return nc, build(nc, io, B, S, totals)

    _, totals = program({})
    nc, again = program(totals)
    assert again == totals
    r = _run(nc, [{f"in_{n}": a for n, a in host.items()}], core_ids=[0])
    return r.results[0]["out_0"]
```
